# Optimizing a Trainium2 kernel written in Bass

```python
import numpy as np
import jax
import jax.numpy as jnp

def _softmax(x, axis=-1):
    return jax.nn.softmax(x, axis=axis)

def _gelu(x):
    return jax.nn.gelu(x, approximate=True)

def _silu(x):
    return jax.nn.silu(x)

def _sigmoid(x):
    return jax.nn.sigmoid(x)

def _layernorm(x, axis=-1, eps=1e-05):
    m = jnp.mean(x, axis=axis, keepdims=True)
    v = jnp.var(x, axis=axis, keepdims=True)
    return (x - m) / jnp.sqrt(v + eps)

def _scatter_add(tgt, idx, src, axis=0):
    return tgt.at[idx].add(src)

def _segment_sum(src, seg, n):
    return jax.ops.segment_sum(src, seg, n)
kernel_name = 'mk_prb_d4_jaxref_r8_adea3e'

def setup_inputs(seed: int=0):
    np.random.seed(seed)
    _w = jnp.asarray

    def _L0_attn_setup():
        import jax, jax.numpy as jnp
        import numpy as np
        DIM, H, KV, HD, WIN = (128, 16, 4, 64, 64)
        EPS = 1e-06

        def rmsnorm(x, w, eps=EPS):
            return x * jax.lax.rsqrt(jnp.mean(x * x, axis=-1, keepdims=True) + eps) * w
        key = jax.random.key(seed)
        ks = jax.random.split(key, 7)
        B, T = (4, 256)
        s = 0.02
        return {'x': jax.random.normal(ks[0], (B, T, DIM), dtype=jnp.float32), 'wq': jax.random.normal(ks[1], (H * HD, DIM), dtype=jnp.float32) * s, 'wk': jax.random.normal(ks[2], (KV * HD, DIM), dtype=jnp.float32) * s, 'wv': jax.random.normal(ks[3], (KV * HD, DIM), dtype=jnp.float32) * s, 'wo': jax.random.normal(ks[4], (DIM, H * HD), dtype=jnp.float32) * s, 'q_norm_w': jnp.ones((HD,), dtype=jnp.float32), 'k_norm_w': jnp.ones((HD,), dtype=jnp.float32)}
    _L0_attn_in = _L0_attn_setup()

    def _L0_ffn_setup():
        import jax, jax.numpy as jnp
        import numpy as np
        S, B, H = (256, 1, 128)
        N_HEADS = 16
        HEAD_DIM = H // N_HEADS
        E, K, F = (8, 2, 256)
        EPS = 1e-05

        def layernorm(x, w, b):
            mu = jnp.mean(x, axis=-1, keepdims=True)
            var = jnp.mean(jnp.square(x - mu), axis=-1, keepdims=True)
            return (x - mu) * jax.lax.rsqrt(var + EPS) * w + b
        key = jax.random.key(seed)
        ks = jax.random.split(key, 8)
        std = 0.02
        return {'x': jax.random.normal(ks[0], (S, B, H), dtype=jnp.float32), 'ln1_w': jnp.ones((H,), jnp.float32), 'ln1_b': jnp.zeros((H,), jnp.float32), 'in_proj_w': jax.random.normal(ks[1], (3 * H, H), jnp.float32) * std, 'in_proj_b': jnp.zeros((3 * H,), jnp.float32), 'out_proj_w': jax.random.normal(ks[2], (H, H), jnp.float32) * std, 'out_proj_b': jnp.zeros((H,), jnp.float32), 'ln2_w': jnp.ones((H,), jnp.float32), 'ln2_b': jnp.zeros((H,), jnp.float32), 'router_w': jax.random.normal(ks[3], (E, H), jnp.float32) * std, 'w1': jax.random.normal(ks[4], (E, H, F), jnp.float32) * std, 'w2': jax.random.normal(ks[5], (E, F, H), jnp.float32) * std}
    _L0_ffn_in = _L0_ffn_setup()

    def _L1_attn_setup():
        import jax, jax.numpy as jnp
        import numpy as np
        import math
        B, S, DIM = (1, 256, 128)
        H, KVH = (16, 4)
        HD = DIM // H
        KV_DIM = KVH * HD

        def _rms_norm(x):
            eps = jnp.finfo(x.dtype).eps
            return x * jax.lax.rsqrt(jnp.mean(x * x, axis=-1, keepdims=True) + eps)

        def _polar_rotary(seq_len, head_dim, dtype):
            angles = jnp.arange(0, head_dim, 2, dtype=jnp.float32) / head_dim * math.pi
            pos = jnp.arange(seq_len, dtype=jnp.float32)
            radius = 1.0 / (1.0 + pos[:, None] * 0.01)
            ang = pos[:, None] * angles[None, :]
            cos = (radius * jnp.cos(ang)).astype(dtype)
            sin = (radius * jnp.sin(ang)).astype(dtype)
            return (cos[None, None], sin[None, None])

        def _apply_rotary(x, cos, sin):
            half = x.shape[-1] // 2
            x1, x2 = (x[..., :half], x[..., half:])
            return jnp.concatenate([x1 * cos + x2 * sin, x1 * -sin + x2 * cos], axis=-1)

        def _causal_attn(q, k, v, scale, mask):
            s = jnp.einsum('bhqd,bhkd->bhqk', q, k) * scale
            s = jnp.where(mask, s, jnp.finfo(s.dtype).min)
            p = jax.nn.softmax(s, axis=-1)
            return jnp.einsum('bhqk,bhkd->bhqd', p, v)
        key = jax.random.key(seed)
        ks = jax.random.split(key, 8)
        std = 0.02
        return {'x': jax.random.normal(ks[0], (B, S, DIM), jnp.float32), 'Wq': jax.random.normal(ks[1], (DIM, DIM), jnp.float32) * std, 'Wk': jax.random.normal(ks[2], (KV_DIM, DIM), jnp.float32) * std, 'Wv': jax.random.normal(ks[3], (KV_DIM, DIM), jnp.float32) * std, 'Wg': jax.random.normal(ks[4], (KV_DIM, DIM), jnp.float32) * std, 'Wo': jax.random.normal(ks[5], (DIM, DIM), jnp.float32) * std, 'q_gain': jnp.full((H,), 1.0, jnp.float32), 'lambda_param': jnp.full((H,), 0.5, jnp.float32)}
    _L1_attn_in = _L1_attn_setup()

    def _L1_ffn_setup():
        import jax, jax.numpy as jnp
        import numpy as np
        H = 128
        I = 352
        E = 8
        TOP_K = 2

        def _moe(hidden_states, router_w, gate_w, up_w, down_w):
            B, S, Hd = hidden_states.shape
            x = hidden_states.reshape(-1, Hd)
            logits = x @ router_w.T
            probs = jax.nn.softmax(logits.astype(jnp.float32), axis=-1)
            top_w, top_idx = jax.lax.top_k(probs, TOP_K)
            top_w = top_w.astype(x.dtype)
            onehot = jax.nn.one_hot(top_idx, E, dtype=x.dtype)
            w_te = jnp.einsum('tk,tke->te', top_w, onehot)
            g = jnp.einsum('th,eih->tei', x, gate_w)
            u = jnp.einsum('th,eih->tei', x, up_w)
            h = jax.nn.silu(g) * u
            y = jnp.einsum('tei,ehi,te->th', h, down_w, w_te)
            return y.reshape(B, S, Hd)
        key = jax.random.key(seed)
        ks = jax.random.split(key, 5)
        s = 0.02
        return {'hidden_states': jax.random.normal(ks[0], (2, 128, H), dtype=jnp.float32), 'router_w': jax.random.normal(ks[1], (E, H), dtype=jnp.float32) * s, 'gate_w': jax.random.normal(ks[2], (E, I, H), dtype=jnp.float32) * s, 'up_w': jax.random.normal(ks[3], (E, I, H), dtype=jnp.float32) * s, 'down_w': jax.random.normal(ks[4], (E, H, I), dtype=jnp.float32) * s}
    _L1_ffn_in = _L1_ffn_setup()

    def _L2_attn_setup():
        import jax, jax.numpy as jnp
        import numpy as np
        EMBED_DIM = 128
        NUM_HEADS = 16
        HEAD_DIM = EMBED_DIM // NUM_HEADS
        key = jax.random.key(seed)
        ks = jax.random.split(key, 9)
        B, S, D = (4, 256, EMBED_DIM)
        s = 1.0 / np.sqrt(D)
        return {'x': jax.random.normal(ks[0], (B, S, D), dtype=jnp.float32), 'Wq': jax.random.uniform(ks[1], (D, D), jnp.float32, -s, s), 'bq': jax.random.uniform(ks[2], (D,), jnp.float32, -s, s), 'Wk': jax.random.uniform(ks[3], (D, D), jnp.float32, -s, s), 'bk': jax.random.uniform(ks[4], (D,), jnp.float32, -s, s), 'Wv': jax.random.uniform(ks[5], (D, D), jnp.float32, -s, s), 'bv': jax.random.uniform(ks[6], (D,), jnp.float32, -s, s), 'Wo': jax.random.uniform(ks[7], (D, D), jnp.float32, -s, s), 'bo': jax.random.uniform(ks[8], (D,), jnp.float32, -s, s)}
    _L2_attn_in = _L2_attn_setup()

    def _L2_ffn_setup():
        import jax, jax.numpy as jnp
        import numpy as np
        B, S, IN, OUT, E, R = (8, 512, 128, 128, 8, 8)
        LORA_ALPHA = 16
        SCALING = LORA_ALPHA / R
        key = jax.random.key(seed)
        k = jax.random.split(key, 6)
        x = jax.random.normal(k[0], (B, S, IN), dtype=jnp.float32)
        base_w = jax.random.normal(k[1], (OUT, IN), dtype=jnp.float32) * 0.02
        base_b = jnp.zeros((OUT,), dtype=jnp.float32)
        lora_A = jax.random.normal(k[2], (IN, R), dtype=jnp.float32) * 0.02
        lora_B = jax.random.normal(k[3], (E, R, OUT), dtype=jnp.float32) * 0.02
        router_w = jax.random.normal(k[4], (E, IN), dtype=jnp.float32) * 0.02
        router_b = jnp.zeros((E,), dtype=jnp.float32)
        return {'x': x, 'base_w': base_w, 'base_b': base_b, 'lora_A': lora_A, 'lora_B': lora_B, 'router_w': router_w, 'router_b': router_b}
    _L2_ffn_in = _L2_ffn_setup()

    def _L3_attn_setup():
        import jax, jax.numpy as jnp
        import numpy as np
        B, L, D_MODEL, H = (4, 256, 128, 16)
        HD = D_MODEL // H
        EPS = 1e-06
        key = jax.random.key(seed)
        ks = jax.random.split(key, 9)
        s = 1.0 / np.sqrt(D_MODEL)
        return {'x': jax.random.normal(ks[0], (B, L, D_MODEL), dtype=jnp.float32), 'Wq': jax.random.normal(ks[1], (D_MODEL, D_MODEL), dtype=jnp.float32) * s, 'bq': jax.random.normal(ks[2], (D_MODEL,), dtype=jnp.float32) * 0.01, 'Wk': jax.random.normal(ks[3], (D_MODEL, D_MODEL), dtype=jnp.float32) * s, 'bk': jax.random.normal(ks[4], (D_MODEL,), dtype=jnp.float32) * 0.01, 'Wv': jax.random.normal(ks[5], (D_MODEL, D_MODEL), dtype=jnp.float32) * s, 'bv': jax.random.normal(ks[6], (D_MODEL,), dtype=jnp.float32) * 0.01, 'Wo': jax.random.normal(ks[7], (D_MODEL, D_MODEL), dtype=jnp.float32) * s, 'bo': jax.random.normal(ks[8], (D_MODEL,), dtype=jnp.float32) * 0.01}
    _L3_attn_in = _L3_attn_setup()

    def _L3_ffn_setup():
        import jax, jax.numpy as jnp
        import numpy as np
        DIM = 128
        HIDDEN = 384
        SCALE = 1.0 / 127.0

        def _dequant(w_int, dtype):
            return w_int.astype(dtype) * jnp.asarray(SCALE, dtype)
        key = jax.random.key(seed)
        k_x, k_g, k_u, k_d = jax.random.split(key, 4)
        x = jax.random.normal(k_x, (4, 256, DIM), dtype=jnp.float32)
        w_gate = jax.random.randint(k_g, (HIDDEN, DIM), -127, 128, dtype=jnp.int32)
        w_up = jax.random.randint(k_u, (HIDDEN, DIM), -127, 128, dtype=jnp.int32)
        w_down = jax.random.randint(k_d, (DIM, HIDDEN), -127, 128, dtype=jnp.int32)
        return {'x': x, 'w_gate': w_gate, 'w_up': w_up, 'w_down': w_down}
    _L3_ffn_in = _L3_ffn_setup()
    _d = {'L0_attn_x': _L0_attn_in['x'], 'L0_attn_wq': _L0_attn_in['wq'], 'L0_attn_wk': _L0_attn_in['wk'], 'L0_attn_wv': _L0_attn_in['wv'], 'L0_attn_wo': _L0_attn_in['wo'], 'L0_attn_q_norm_w': _L0_attn_in['q_norm_w'], 'L0_attn_k_norm_w': _L0_attn_in['k_norm_w'], 'L0_ffn_ln1_w': _L0_ffn_in['ln1_w'], 'L0_ffn_ln1_b': _L0_ffn_in['ln1_b'], 'L0_ffn_in_proj_w': _L0_ffn_in['in_proj_w'], 'L0_ffn_in_proj_b': _L0_ffn_in['in_proj_b'], 'L0_ffn_out_proj_w': _L0_ffn_in['out_proj_w'], 'L0_ffn_out_proj_b': _L0_ffn_in['out_proj_b'], 'L0_ffn_ln2_w': _L0_ffn_in['ln2_w'], 'L0_ffn_ln2_b': _L0_ffn_in['ln2_b'], 'L0_ffn_router_w': _L0_ffn_in['router_w'], 'L0_ffn_w1': _L0_ffn_in['w1'], 'L0_ffn_w2': _L0_ffn_in['w2'], 'L1_attn_Wq': _L1_attn_in['Wq'], 'L1_attn_Wk': _L1_attn_in['Wk'], 'L1_attn_Wv': _L1_attn_in['Wv'], 'L1_attn_Wg': _L1_attn_in['Wg'], 'L1_attn_Wo': _L1_attn_in['Wo'], 'L1_attn_q_gain': _L1_attn_in['q_gain'], 'L1_attn_lambda_param': _L1_attn_in['lambda_param'], 'L1_ffn_router_w': _L1_ffn_in['router_w'], 'L1_ffn_gate_w': _L1_ffn_in['gate_w'], 'L1_ffn_up_w': _L1_ffn_in['up_w'], 'L1_ffn_down_w': _L1_ffn_in['down_w'], 'L2_attn_Wq': _L2_attn_in['Wq'], 'L2_attn_bq': _L2_attn_in['bq'], 'L2_attn_Wk': _L2_attn_in['Wk'], 'L2_attn_bk': _L2_attn_in['bk'], 'L2_attn_Wv': _L2_attn_in['Wv'], 'L2_attn_bv': _L2_attn_in['bv'], 'L2_attn_Wo': _L2_attn_in['Wo'], 'L2_attn_bo': _L2_attn_in['bo'], 'L2_ffn_base_w': _L2_ffn_in['base_w'], 'L2_ffn_base_b': _L2_ffn_in['base_b'], 'L2_ffn_lora_A': _L2_ffn_in['lora_A'], 'L2_ffn_lora_B': _L2_ffn_in['lora_B'], 'L2_ffn_router_w': _L2_ffn_in['router_w'], 'L2_ffn_router_b': _L2_ffn_in['router_b'], 'L3_attn_Wq': _L3_attn_in['Wq'], 'L3_attn_bq': _L3_attn_in['bq'], 'L3_attn_Wk': _L3_attn_in['Wk'], 'L3_attn_bk': _L3_attn_in['bk'], 'L3_attn_Wv': _L3_attn_in['Wv'], 'L3_attn_bv': _L3_attn_in['bv'], 'L3_attn_Wo': _L3_attn_in['Wo'], 'L3_attn_bo': _L3_attn_in['bo'], 'L3_ffn_w_gate': _L3_ffn_in['w_gate'], 'L3_ffn_w_up': _L3_ffn_in['w_up'], 'L3_ffn_w_down': _L3_ffn_in['w_down']}
    _x0 = _d['L0_attn_x']
    _d['L0_attn_x'] = jax.random.normal(jax.random.fold_in(jax.random.key(seed), 1), (4, 512, 128), dtype=_x0.dtype)
    del _x0
    return _d

def reference(L0_attn_x, L0_attn_wq, L0_attn_wk, L0_attn_wv, L0_attn_wo, L0_attn_q_norm_w, L0_attn_k_norm_w, L0_ffn_ln1_w, L0_ffn_ln1_b, L0_ffn_in_proj_w, L0_ffn_in_proj_b, L0_ffn_out_proj_w, L0_ffn_out_proj_b, L0_ffn_ln2_w, L0_ffn_ln2_b, L0_ffn_router_w, L0_ffn_w1, L0_ffn_w2, L1_attn_Wq, L1_attn_Wk, L1_attn_Wv, L1_attn_Wg, L1_attn_Wo, L1_attn_q_gain, L1_attn_lambda_param, L1_ffn_router_w, L1_ffn_gate_w, L1_ffn_up_w, L1_ffn_down_w, L2_attn_Wq, L2_attn_bq, L2_attn_Wk, L2_attn_bk, L2_attn_Wv, L2_attn_bv, L2_attn_Wo, L2_attn_bo, L2_ffn_base_w, L2_ffn_base_b, L2_ffn_lora_A, L2_ffn_lora_B, L2_ffn_router_w, L2_ffn_router_b, L3_attn_Wq, L3_attn_bq, L3_attn_Wk, L3_attn_bk, L3_attn_Wv, L3_attn_bv, L3_attn_Wo, L3_attn_bo, L3_ffn_w_gate, L3_ffn_w_up, L3_ffn_w_down):

    def _L0_attn_ref(x, wq, wk, wv, wo, q_norm_w, k_norm_w):
        import jax, jax.numpy as jnp
        import numpy as np
        DIM, H, KV, HD, WIN = (128, 16, 4, 64, 64)
        EPS = 1e-06

        def rmsnorm(x, w, eps=EPS):
            return x * jax.lax.rsqrt(jnp.mean(x * x, axis=-1, keepdims=True) + eps) * w
        B, T, D = x.shape
        rep = H // KV
        q = (x @ wq.T).reshape(B, T, H, HD)
        k = (x @ wk.T).reshape(B, T, KV, HD)
        v = (x @ wv.T).reshape(B, T, KV, HD)
        q = rmsnorm(q, q_norm_w)
        k = rmsnorm(k, k_norm_w)
        k = jnp.repeat(k, rep, axis=2)
        v = jnp.repeat(v, rep, axis=2)
        scores = jnp.einsum('bqhd,bkhd->bhqk', q, k) / jnp.sqrt(jnp.float32(HD))
        i = jnp.arange(T)[:, None]
        j = jnp.arange(T)[None, :]
        mask = (i >= j) & (i - j < WIN)
        scores = jnp.where(mask, scores, -jnp.inf)
        attn = jax.nn.softmax(scores, axis=-1)
        y = jnp.einsum('bhqk,bkhd->bqhd', attn, v).reshape(B, T, H * HD)
        return y @ wo.T

    def _L0_ffn_ref(x, ln1_w, ln1_b, in_proj_w, in_proj_b, out_proj_w, out_proj_b, ln2_w, ln2_b, router_w, w1, w2):
        import jax, jax.numpy as jnp
        import numpy as np
        S, B, H = (256, 1, 128)
        N_HEADS = 16
        HEAD_DIM = H // N_HEADS
        E, K, F = (8, 2, 256)
        EPS = 1e-05

        def layernorm(x, w, b):
            mu = jnp.mean(x, axis=-1, keepdims=True)
            var = jnp.mean(jnp.square(x - mu), axis=-1, keepdims=True)
            return (x - mu) * jax.lax.rsqrt(var + EPS) * w + b
        s, b, h = x.shape
        hn = layernorm(x, ln1_w, ln1_b)
        qkv = hn @ in_proj_w.T + in_proj_b
        q, k, v = jnp.split(qkv, 3, axis=-1)
        q = q.reshape(s, b, N_HEADS, HEAD_DIM)
        k = k.reshape(s, b, N_HEADS, HEAD_DIM)
        v = v.reshape(s, b, N_HEADS, HEAD_DIM)
        scores = jnp.einsum('sbnd,tbnd->bnst', q, k) / np.sqrt(HEAD_DIM)
        causal = jnp.tril(jnp.ones((s, s), bool))
        scores = jnp.where(causal[None, None], scores, -jnp.inf)
        probs = jax.nn.softmax(scores, axis=-1)
        attn = jnp.einsum('bnst,tbnd->sbnd', probs, v).reshape(s, b, h)
        attn = attn @ out_proj_w.T + out_proj_b
        x1 = x + attn
        hn2 = layernorm(x1, ln2_w, ln2_b).reshape(s * b, h)
        logits = hn2 @ router_w.T
        rp = jax.nn.softmax(logits, axis=-1)
        topw, topi = jax.lax.top_k(rp, K)
        gates = jnp.sum(jax.nn.one_hot(topi, E, dtype=hn2.dtype) * topw[..., None], axis=1)
        hmid = jax.nn.gelu(jnp.einsum('th,ehf->tef', hn2, w1), approximate=False)
        y = jnp.einsum('tef,efh->th', hmid * gates[:, :, None], w2)
        return x1 + y.reshape(s, b, h)

    def _L1_attn_ref(x, Wq, Wk, Wv, Wg, Wo, q_gain, lambda_param):
        import jax, jax.numpy as jnp
        import numpy as np
        import math
        B, S, DIM = (1, 256, 128)
        H, KVH = (16, 4)
        HD = DIM // H
        KV_DIM = KVH * HD

        def _rms_norm(x):
            eps = jnp.finfo(x.dtype).eps
            return x * jax.lax.rsqrt(jnp.mean(x * x, axis=-1, keepdims=True) + eps)

        def _polar_rotary(seq_len, head_dim, dtype):
            angles = jnp.arange(0, head_dim, 2, dtype=jnp.float32) / head_dim * math.pi
            pos = jnp.arange(seq_len, dtype=jnp.float32)
            radius = 1.0 / (1.0 + pos[:, None] * 0.01)
            ang = pos[:, None] * angles[None, :]
            cos = (radius * jnp.cos(ang)).astype(dtype)
            sin = (radius * jnp.sin(ang)).astype(dtype)
            return (cos[None, None], sin[None, None])

        def _apply_rotary(x, cos, sin):
            half = x.shape[-1] // 2
            x1, x2 = (x[..., :half], x[..., half:])
            return jnp.concatenate([x1 * cos + x2 * sin, x1 * -sin + x2 * cos], axis=-1)

        def _causal_attn(q, k, v, scale, mask):
            s = jnp.einsum('bhqd,bhkd->bhqk', q, k) * scale
            s = jnp.where(mask, s, jnp.finfo(s.dtype).min)
            p = jax.nn.softmax(s, axis=-1)
            return jnp.einsum('bhqk,bhkd->bhqd', p, v)
        bsz, seqlen, dim = x.shape
        q = (x @ Wq.T).reshape(bsz, seqlen, H, HD).transpose(0, 2, 1, 3)
        k = (x @ Wk.T).reshape(bsz, seqlen, KVH, HD).transpose(0, 2, 1, 3)
        v = (x @ Wv.T).reshape(bsz, seqlen, KVH, HD).transpose(0, 2, 1, 3)
        v_g = jax.nn.sigmoid((x @ Wg.T).reshape(bsz, seqlen, KVH, HD).transpose(0, 2, 1, 3))
        v = v * v_g
        q = _rms_norm(q)
        k = _rms_norm(k)
        cos, sin = _polar_rotary(seqlen, HD, q.dtype)
        q = _apply_rotary(q, cos, sin)
        k = _apply_rotary(k, cos, sin)
        q = q * q_gain.astype(q.dtype)[None, :, None, None]
        rep = H // KVH
        k = jnp.repeat(k, rep, axis=1)
        v = jnp.repeat(v, rep, axis=1)
        half = HD // 2
        q1, q2 = (q[..., :half], q[..., half:])
        k1, k2 = (k[..., :half], k[..., half:])
        v1, v2 = (v[..., :half], v[..., half:])
        scale = 1.0 / math.sqrt(half)
        mask = jnp.tril(jnp.ones((seqlen, seqlen), dtype=bool))[None, None]
        a1 = _causal_attn(q1, k1, v1, scale, mask)
        a2 = _causal_attn(q2, k2, v2, scale, mask)
        lp = lambda_param.astype(q.dtype)[None, :, None, None]
        y = jnp.concatenate([a1 - lp * a2, a1 + lp * a2], axis=-1)
        y = y.transpose(0, 2, 1, 3).reshape(bsz, seqlen, dim)
        return y @ Wo.T

    def _L1_ffn_ref(hidden_states, router_w, gate_w, up_w, down_w):
        import jax, jax.numpy as jnp
        import numpy as np
        H = 128
        I = 352
        E = 8
        TOP_K = 2

        def _moe(hidden_states, router_w, gate_w, up_w, down_w):
            B, S, Hd = hidden_states.shape
            x = hidden_states.reshape(-1, Hd)
            logits = x @ router_w.T
            probs = jax.nn.softmax(logits.astype(jnp.float32), axis=-1)
            top_w, top_idx = jax.lax.top_k(probs, TOP_K)
            top_w = top_w.astype(x.dtype)
            onehot = jax.nn.one_hot(top_idx, E, dtype=x.dtype)
            w_te = jnp.einsum('tk,tke->te', top_w, onehot)
            g = jnp.einsum('th,eih->tei', x, gate_w)
            u = jnp.einsum('th,eih->tei', x, up_w)
            h = jax.nn.silu(g) * u
            y = jnp.einsum('tei,ehi,te->th', h, down_w, w_te)
            return y.reshape(B, S, Hd)
        return _moe(hidden_states, router_w, gate_w, up_w, down_w)

    def _L2_attn_ref(x, Wq, bq, Wk, bk, Wv, bv, Wo, bo):
        import jax, jax.numpy as jnp
        import numpy as np
        EMBED_DIM = 128
        NUM_HEADS = 16
        HEAD_DIM = EMBED_DIM // NUM_HEADS
        B, S, D = x.shape
        H, Hd = (NUM_HEADS, HEAD_DIM)

        def proj(W, b):
            y = jnp.einsum('bsd,ed->bse', x, W) + b
            return y.reshape(B, S, H, Hd).transpose(0, 2, 1, 3)
        Q = proj(Wq, bq)
        K = proj(Wk, bk)
        V = proj(Wv, bv)
        scores = jnp.einsum('bhqd,bhkd->bhqk', Q, K) / np.sqrt(Hd).astype(jnp.float32)
        attn = jax.nn.softmax(scores, axis=-1)
        out = jnp.einsum('bhqk,bhkd->bhqd', attn, V)
        out = out.transpose(0, 2, 1, 3).reshape(B, S, D)
        return jnp.einsum('bsd,ed->bse', out, Wo) + bo

    def _L2_ffn_ref(x, base_w, base_b, lora_A, lora_B, router_w, router_b):
        import jax, jax.numpy as jnp
        import numpy as np
        B, S, IN, OUT, E, R = (8, 512, 128, 128, 8, 8)
        LORA_ALPHA = 16
        SCALING = LORA_ALPHA / R
        result = jnp.einsum('bsd,od->bso', x, base_w) + base_b
        logits = jnp.einsum('bsd,ed->bse', x, router_w) + router_b
        gating = jax.nn.softmax(logits, axis=-1).astype(jnp.bfloat16)
        mid = jnp.einsum('bsd,dr->bsr', x, lora_A)
        lora_out = jnp.einsum('bsr,erd,bse->bsd', mid, lora_B, gating.astype(jnp.float32))
        return result + lora_out * SCALING

    def _L3_attn_ref(x, Wq, bq, Wk, bk, Wv, bv, Wo, bo):
        import jax, jax.numpy as jnp
        import numpy as np
        B, L, D_MODEL, H = (4, 256, 128, 16)
        HD = D_MODEL // H
        EPS = 1e-06
        b, l, _ = x.shape
        s = l

        def proj(W, bias):
            return (x @ W.T + bias).reshape(b, l, H, HD).transpose(0, 2, 1, 3)
        q = jax.nn.sigmoid(proj(Wq, bq))
        k = jax.nn.sigmoid(proj(Wk, bk))
        v = proj(Wv, bv)
        sink_incoming = 1.0 / jnp.einsum('nhld,nhd->nhl', q + EPS, k.sum(axis=2) + EPS)
        source_outgoing = 1.0 / jnp.einsum('nhld,nhd->nhl', k + EPS, q.sum(axis=2) + EPS)
        conserved_sink = jnp.einsum('nhld,nhd->nhl', q + EPS, (k * source_outgoing[..., None]).sum(axis=2) + EPS)
        conserved_source = jnp.einsum('nhld,nhd->nhl', k + EPS, (q * sink_incoming[..., None]).sum(axis=2) + EPS)
        conserved_source = jnp.clip(conserved_source, -1.0, 1.0)
        sink_allocation = jax.nn.sigmoid(conserved_sink * (float(l) / float(s)))
        source_competition = jax.nn.softmax(conserved_source, axis=-1) * float(s)
        kv = jnp.einsum('nhld,nhlm->nhdm', k, v * source_competition[..., None])
        out = jnp.einsum('nhld,nhdm->nhlm', q * sink_incoming[..., None], kv)
        out = out * sink_allocation[..., None]
        out = out.transpose(0, 2, 1, 3).reshape(b, l, D_MODEL)
        return out @ Wo.T + bo

    def _L3_ffn_ref(x, w_gate, w_up, w_down):
        import jax, jax.numpy as jnp
        import numpy as np
        DIM = 128
        HIDDEN = 384
        SCALE = 1.0 / 127.0

        def _dequant(w_int, dtype):
            return w_int.astype(dtype) * jnp.asarray(SCALE, dtype)
        wg = _dequant(w_gate, x.dtype)
        wu = _dequant(w_up, x.dtype)
        wd = _dequant(w_down, x.dtype)
        gate = jnp.einsum('bsd,hd->bsh', x, wg)
        up = jnp.einsum('bsd,hd->bsh', x, wu)
        h = jax.nn.silu(gate) * up
        return jnp.einsum('bsh,dh->bsd', h, wd)
    x = L0_attn_x
    xn = _layernorm(x, axis=-1)
    x = x + _L0_attn_ref(xn, L0_attn_wq, L0_attn_wk, L0_attn_wv, L0_attn_wo, L0_attn_q_norm_w, L0_attn_k_norm_w) + _L0_ffn_ref(xn, L0_ffn_ln1_w, L0_ffn_ln1_b, L0_ffn_in_proj_w, L0_ffn_in_proj_b, L0_ffn_out_proj_w, L0_ffn_out_proj_b, L0_ffn_ln2_w, L0_ffn_ln2_b, L0_ffn_router_w, L0_ffn_w1, L0_ffn_w2)
    xn = _layernorm(x, axis=-1)
    x = x + _L1_attn_ref(xn, L1_attn_Wq, L1_attn_Wk, L1_attn_Wv, L1_attn_Wg, L1_attn_Wo, L1_attn_q_gain, L1_attn_lambda_param) + _L1_ffn_ref(xn, L1_ffn_router_w, L1_ffn_gate_w, L1_ffn_up_w, L1_ffn_down_w)
    xn = _layernorm(x, axis=-1)
    x = x + _L2_attn_ref(xn, L2_attn_Wq, L2_attn_bq, L2_attn_Wk, L2_attn_bk, L2_attn_Wv, L2_attn_bv, L2_attn_Wo, L2_attn_bo) + _L2_ffn_ref(xn, L2_ffn_base_w, L2_ffn_base_b, L2_ffn_lora_A, L2_ffn_lora_B, L2_ffn_router_w, L2_ffn_router_b)
    xn = _layernorm(x, axis=-1)
    x = x + _L3_attn_ref(xn, L3_attn_Wq, L3_attn_bq, L3_attn_Wk, L3_attn_bk, L3_attn_Wv, L3_attn_bv, L3_attn_Wo, L3_attn_bo) + _L3_ffn_ref(xn, L3_ffn_w_gate, L3_ffn_w_up, L3_ffn_w_down)
    return x

_drawn_inputs = setup_inputs


def setup_inputs(seed=0):
    import zlib

    import numpy as np

    out = dict(_drawn_inputs(seed))
    spreads = {'L0_attn_q_norm_w': (1.0, 0.6),
     'L0_attn_k_norm_w': (1.0, 0.6),
     'L0_ffn_ln1_w': (1.0, 0.6),
     'L0_ffn_ln1_b': (0.0, 0.8),
     'L0_ffn_in_proj_b': (0.0, 0.46),
     'L0_ffn_out_proj_b': (0.0, 0.1),
     'L0_ffn_ln2_w': (1.0, 0.6),
     'L0_ffn_ln2_b': (0.0, 0.8),
     'L1_attn_q_gain': (1.0, 0.6),
     'L1_attn_lambda_param': (0.5, 0.6),
     'L2_ffn_base_b': (0.0, 0.324),
     'L2_ffn_router_b': (0.0, 0.8)}
    factors = {'L0_attn_wq': 3.017,
     'L0_attn_wk': 3.014,
     'L0_ffn_router_w': 8.0,
     'L0_ffn_w1': 8.0,
     'L0_ffn_w2': 8.0,
     'L1_attn_Wq': 8.0,
     'L1_attn_Wk': 8.0,
     'L1_attn_Wv': 8.0,
     'L1_attn_Wg': 8.0,
     'L1_attn_Wo': 8.0,
     'L1_ffn_router_w': 8.0,
     'L1_ffn_gate_w': 8.0,
     'L1_ffn_up_w': 8.0,
     'L1_ffn_down_w': 8.0,
     'L2_attn_Wq': 6.943,
     'L2_attn_bq': 8.0,
     'L2_attn_Wk': 7.041,
     'L2_attn_bk': 200.0,
     'L2_attn_Wv': 3.145,
     'L2_attn_bv': 7.941,
     'L2_ffn_lora_A': 8.0,
     'L2_ffn_lora_B': 8.0,
     'L2_ffn_router_w': 8.0,
     'L3_attn_Wq': 200.0,
     'L3_attn_bq': 200.0,
     'L3_attn_Wk': 200.0,
     'L3_attn_bk': 200.0,
     'L3_attn_Wv': 8.0,
     'L3_attn_bv': 200.0,
     'L3_attn_Wo': 8.0,
     'L3_attn_bo': 200.0,
     'L2_attn_bo': 4.547}
    for name, (base, spread) in spreads.items():
        noise = np.random.default_rng([zlib.crc32(name.encode()), seed]).standard_normal(out[name].shape)
        drawn = base * np.exp(spread * noise) if base else spread * noise
        out[name] = jnp.asarray(drawn.astype(out[name].dtype))
    for name, factor in factors.items():
        out[name] = (out[name] * factor).astype(out[name].dtype)
    return out
```

```python
import math
from contextlib import ExitStack

import numpy as np
import concourse.bass as bass
from concourse import mybir

F32 = mybir.dt.float32
BF16 = mybir.dt.bfloat16
I32 = mybir.dt.int32
ALU = mybir.AluOpType
ACT = mybir.ActivationFunctionType
AX = mybir.AxisListType

P = 128
NB = 4
T = 512
NT = NB * T
NEG = -1e30
PE, AC, DV, PO, SY = "tensor", "scalar", "vector", "gpsimd", "sync"
QT = ("h", "h", "m", "m", "h", "l")
KT = ("h", "m", "h", "m", "l", "h")
PART = {"h": 0, "m": 1, "l": 2}


class Op:

    def __init__(self, eng, fn, waits):
        self.eng, self.fn, self.waits = eng, fn, waits
        self.flag, self.sem, self.val = False, None, 0


class Landed:

    def __init__(self, sem, val):
        self.sem, self.val = sem, val


class Queues:

    def __init__(self, nc, ctx):
        self.nc, self.ctx = nc, ctx
        self.q = {e: [] for e in (PE, AC, DV, PO, SY)}
        self.sem = {e: ctx.enter_context(nc.semaphore("done_" + e)) for e in (PE, AC, DV, PO)}
        self.dma_sems = {}

    def op(self, eng, fn, *waits):
        flat = []

        def add(w):
            if w is None:
                return
            if isinstance(w, (list, tuple)):
                for x in w:
                    add(x)
                return
            if isinstance(w, Op):
                w.flag = True
            flat.append(w)

        add(waits)
        o = Op(eng, fn, flat)
        self.q[eng].append(o)
        return o

    def dma(self, name, out, in_, *waits, eng=SY):
        if name not in self.dma_sems:
            self.dma_sems[name] = [self.ctx.enter_context(self.nc.semaphore("dma_" + name)), 0]
        s = self.dma_sems[name]
        s[1] += 16
        o = self.op(eng, lambda e: e.dma_start(out, in_), *waits)
        o.sem = s[0]
        return Landed(s[0], s[1])

    def emit(self):
        for e in (PE, AC, DV, PO):
            n = 0
            for o in self.q[e]:
                if o.flag and o.sem is None:
                    n += 1
                    o.val = n
        block = self.ctx.enter_context(self.nc.Block())
        for name in (SY, PE, AC, DV, PO):
            def body(eng, name=name):
                seen = {}
                for o in self.q[name]:
                    need = {}
                    for w in o.waits:
                        s = w.sem if isinstance(w, Landed) else self.sem[w.eng]
                        need[id(s)] = (s, max(w.val, need.get(id(s), (s, 0))[1]))
                    for k, (s, v) in need.items():
                        if seen.get(k, 0) < v:
                            eng.wait_ge(s, v)
                            seen[k] = v
                    ins = o.fn(eng)
                    if o.sem is not None:
                        ins.then_inc(o.sem, 16)
                    elif o.flag:
                        ins.then_inc(self.sem[name], 1)
            blocks = {SY: block.sync, PE: block.tensor, AC: block.scalar, DV: block.vector, PO: block.gpsimd}
            blocks[name](body)


class Buf:

    def __init__(self, ap):
        self.ap, self.busy, self._free = ap, False, []

    @property
    def free(self):
        return self._free

    @free.setter
    def free(self, readers):
        self._free, self.busy = readers, False


class Ring:
    def __init__(self, aps):
        self.bufs, self.n = [Buf(a) for a in aps], 0

    def next(self):
        b = self.bufs[self.n % len(self.bufs)]
        self.n += 1
        assert not b.busy, "a buffer is taken before its last use is queued"
        b.busy = True
        return b


def interleave(a, b, ratio):
    due, a_on, b_on = 0.0, True, True
    while a_on or b_on:
        if a_on and next(a, "end") == "end":
            a_on = False
        due += ratio
        while b_on and (due >= 1 or not a_on):
            due -= 1
            if next(b, "end") == "end":
                b_on = False


def build(nc, d, out, layers=(0, 1, 2, 3), parts=("attn", "ffn"), last="x"):
    ctx = ExitStack()
    with ctx:
        Q = Queues(nc, ctx)
        op, dma = Q.op, Q.dma

        def sb(name, shape, dt=F32):
            return ctx.enter_context(nc.sbuf_tensor(name, shape, dt))

        A = [ctx.enter_context(nc.psum_tensor(f"psA{i}", [P, 2, T], F32)) for i in range(2)]
        B = [ctx.enter_context(nc.psum_tensor(f"psB{i}", [P, T], F32)) for i in range(4)]
        pairs = Ring([a[:, :, :] for a in A])
        bankO = Buf(B[0][:, :])
        misc = Ring([B[1][:, :], B[2][:, :]])
        bankY = Buf(B[3][:, :])

        def mm(out, lhsT, rhs, start, stop, *waits):
            return op(PE, lambda e: e.matmul(out, lhsT, rhs, start=start, stop=stop, skip_group_check=True), *waits)

        def tr(out, in_, *waits):
            return op(PE, lambda e: e.transpose(out, in_, ident[0:in_.shape[0], 0:in_.shape[0]]), *waits)

        def act(out, in_, f, *waits, bias=0.0, scale=1.0, accum=None):
            kw = {} if accum is None else {"accum_out": accum}
            if f == ACT.Copy and bias == 0.0:
                return op(AC, lambda e: e.activation(out, in_, f, scale=scale, **kw), *waits)
            return op(AC, lambda e: e.activation(out, in_, f, bias=bias, scale=scale, **kw), *waits)

        def tt(out, a, b, o, *waits, eng=DV):
            return op(eng, lambda e: e.tensor_tensor(out, a, b, o), *waits)

        def ts(out, a, s1, s2, o1, o2, *waits, eng=DV):
            if s2 is None:
                return op(eng, lambda e: e.tensor_scalar(out, a, s1, None, o1), *waits)
            return op(eng, lambda e: e.tensor_scalar(out, a, s1, s2, o1, o2), *waits)

        def stt(out, a, s, b, o1, o2, *waits):
            return op(DV, lambda e: e.scalar_tensor_tensor(out, a, s, b, o1, o2), *waits)

        def cp(out, a, *waits, eng=DV):
            return op(eng, lambda e: e.tensor_copy(out, a), *waits)

        def red(out, a, o, *waits):
            return op(DV, lambda e: e.tensor_reduce(out, a, AX.X, o), *waits)

        def rec(out, a, *waits):
            return op(DV, lambda e: e.reciprocal(out, a), *waits)

        def fill(out, v, *waits, eng=PO):
            return op(eng, lambda e: e.memset(out, v), *waits)

        W = {}
        L = {}
        wA = sb("wA", [P, 4096])
        w0 = sb("w0", [P, 3328])
        arena = sb("arena", [P, 16384])

        def load(name, dt=F32):
            h = d[name]
            W[name] = sb("w_" + name, list(h.shape), dt)
            full = tuple(slice(None) for _ in h.shape)
            L[name] = dma(name, W[name][full], h.bitcast(BF16) if dt == BF16 else h)

        xT = sb("xT", [P, NT])
        Lx = [dma(f"x{b}", xT[:, b * T:(b + 1) * T], d["xT"][:, b * T:(b + 1) * T]) for b in range(NB)]
        for n in ("ident", "ones", "blk8", "mband", "vecs", "hsel"):
            load(n)
        for n in ("identb", "mdiag", "mdiagT", "selE", "selR"):
            load(n, BF16)
        ident = W["ident"]
        vecs = W["vecs"]
        VEC = {n: i for i, n in enumerate(VECS)}

        def vec(n):
            i = VEC[n]
            return vecs[:, i:i + 1]

        for n in ("ssel", "ohalf", "tril8"):
            load(n)
        if 0 in layers:
            load("rt0")
            o = 0
            for n, sh in (("wq0", (1024,)), ("wk0", (512,)), ("wv0", (256,)), ("wo0", (8, P)), ("inp0", (384,)), ("outp0", (P,))):
                k = int(np.prod(sh))
                v = w0[:, o:o + k]
                W[n] = v if len(sh) == 1 else v.rearrange("p (a c) -> p a c", a=sh[0])
                L[n] = dma(n, W[n], d[n])
                o += k
            W["w1_0"] = wA[:, 0:2048].rearrange("p (e f) -> p e f", e=8)
            W["w2_0"] = wA[:, 2048:4096].rearrange("p (e f) -> p e f", e=16)
            for n in ("w1_0", "w2_0"):
                L[n] = dma(n, W[n], d[n])
        if 1 in layers:
            for n in ("wqk1", "cos1", "sin1", "selq1", "selk1", "wvg1", "wo1", "lp1", "rt1"):
                load(n)
        if 2 in layers:
            for n in ("wq2", "wk2", "wv2", "bv2", "wo2", "base2", "la2", "lb2", "rt2", "rb2"):
                load(n)
        if 3 in layers:
            for n in ("wq3", "wk3", "wv3", "bv3", "wo3"):
                load(n)

        xn = sb("xn", [P, NT])
        res = sb("res", [P, NT])
        pbuf = sb("pbuf", [P, 4, 2, T])
        tA = Ring([sb(f"tA{i}", [P, T])[:, :] for i in range(4)])
        tF = Ring([sb(f"tF{i}", [P, T])[:, :] for i in range(5)])
        tH = Ring([sb(f"tH{i}", [P, T])[:, :] for i in range(3)])
        tG = Ring([sb(f"tG{i}", [P, T])[:, :] for i in range(2)])
        small = Ring([sb(f"sm{i}", [P, 64])[:, :] for i in range(6)])
        state = {"x": [[Lx[b]] for b in range(NB)]}

        def cols(t, b):
            return t[:, b * T:(b + 1) * T]

        def spread(reps, ring, *waits):
            ex = ring.next()
            v = ex.ap.rearrange("p (t r) -> p t r", t=4)
            n, c = 0, None
            for src, rep in reps:
                k = src.shape[2]
                if rep > 0:
                    c = cp(v[:, :, n:n + k * rep].rearrange("p t (k r) -> p t k r", r=rep),
                           src.unsqueeze(3).to_broadcast([P, 4, k, rep]), waits, ex.free)
                else:
                    rep = -rep
                    c = cp(v[:, :, n:n + k * rep].rearrange("p t (r k) -> p t r k", r=rep),
                           src.unsqueeze(2).to_broadcast([P, 4, rep, k]), waits, ex.free)
                n += k * rep
            bk = misc.next()
            for t in range(4):
                m = tr(bk.ap[0:n, t * P:(t + 1) * P], v[:, t, 0:n], c, bk.free, L["ident"])
            ex.free = [m]
            return bk, m

        def lnorm(src, dst, waits, free=(), w=None, bb=None, eps=1e-5):
            b1 = misc.next()
            m = mm(b1.ap, W["ones"][:, :], src, True, True, b1.free, waits, L["ones"])
            xc = tt(dst, src, b1.ap, ALU.subtract, m, free)
            b1.free = [xc]
            s = tA.next()
            sq = act(s.ap, dst, ACT.Square, xc, s.free)
            b2 = misc.next()
            for t in range(4):
                v = mm(b2.ap[:, t:t + 1], s.ap[:, t * P:(t + 1) * P], W["ones"][:, 0:1], True, True, sq, b2.free)
            s.free = [v]
            st = small.next()
            e = ts(st.ap[:, 0:4], b2.ap[:, 0:4], eps, None, ALU.add, None, v, st.free)
            b2.free = [e]
            r = tt(st.ap[:, 4:8], st.ap[:, 0:4], W["ohalf"][:, 0:4], ALU.pow, e, L["ohalf"], eng=PO)
            bk, m = spread([(st.ap[:, 4:8].unsqueeze(2), P)], tA, r)
            st.free = [m]
            if w is None:
                o = tt(dst, dst, bk.ap, ALU.mult, m)
                bk.free = [o]
                return o
            o1 = stt(dst, dst, w, bk.ap, ALU.mult, ALU.mult, m, L["vecs"])
            bk.free = [o1]
            return ts(dst, dst, bb, None, ALU.add, None, o1)

        def softmax8(logits, w, g, ring):
            st = ring.next()
            m4 = st.ap[:, 0:4]
            mx = red(m4, logits, ALU.max, w, st.free)
            sub = tt(logits, logits, m4.unsqueeze(2).to_broadcast([P, 4, 8]), ALU.subtract, mx)
            ex = act(logits, logits, ACT.Exp, sub)
            sm = red(st.ap[:, 4:8], logits, ALU.add, ex)
            rc = rec(st.ap[:, 8:12], st.ap[:, 4:8], sm)
            o = tt(logits, logits, st.ap[:, 8:12].unsqueeze(2).to_broadcast([P, 4, 8]), ALU.mult, rc)
            st.free = [o]
            return o

        gst = sb("gst", [P, 4, 24])
        rk = sb("rk", [P, 32, 8])
        rk2 = sb("rk2", [P, 32, 8])
        gT = Ring([sb(f"gT{i}", [P, T], BF16)[:, :] for i in range(2)])
        gsplit = Ring([sb(f"gsp{i}", [P, 3, 32], BF16)[:, :, :] for i in range(2)])
        gz = [fill(gst[:, :, :], 0.0, eng=DV)]
        for bf in gT.bufs:
            bf.free = [fill(bf.ap, 0.0, eng=DV)]
        gfree = [gz]
        rkfree = [None]

        def route(src, waits, rt, top2, bias=None):
            bk = misc.next()
            for qt in range(4):
                m = mm(bk.ap[:, 8 * qt:8 * qt + 8], src[:, qt * P:(qt + 1) * P], W[rt][:, :], True, True,
                       waits, bk.free, L[rt])
            s = small.next()
            lg = s.ap[:, 0:32].rearrange("p (t e) -> p t e", e=8)
            bv = bk.ap[:, 0:32].rearrange("p (t e) -> p t e", e=8)
            if bias is None:
                c = cp(lg, bv, m, s.free)
            else:
                c = tt(lg, bv, W[bias][:, :].unsqueeze(1).to_broadcast([P, 4, 8]), ALU.add, m, s.free, L[bias])
            bk.free = [c]
            pr = softmax8(lg, c, None, small)
            flat = s.ap[:, 0:32]
            gs = gsplit.next()
            if top2:
                pj = lg.unsqueeze(2).to_broadcast([P, 4, 8, 8])
                pe_ = lg.unsqueeze(3).to_broadcast([P, 4, 8, 8])
                r1 = rk[:, :, :].rearrange("p (t e) j -> p t e j", e=8)
                r2 = rk2[:, :, :].rearrange("p (t e) j -> p t e j", e=8)
                a = [tt(r1[:, t], pj[:, t], pe_[:, t], ALU.is_equal, pr, rkfree) for t in range(4)][-1]
                a2 = tt(rk[:, :, :], rk[:, :, :], W["tril8"][:, :, :], ALU.mult, a, L["tril8"])
                a3 = [tt(r2[:, t], pj[:, t], pe_[:, t], ALU.is_gt, pr, rkfree) for t in range(4)][-1]
                a4 = tt(rk[:, :, :], rk[:, :, :], rk2[:, :, :], ALU.add, a2, a3)
                a5 = red(s.ap[:, 32:64], rk[:, :, :], ALU.add, a4)
                rkfree[0] = a5
                pr = stt(flat, s.ap[:, 32:64], 1.5, flat, ALU.is_lt, ALU.mult, a5)
            h = cp(gs.ap[:, 0, :], flat, pr, gs.free)
            gv = gst[:, :, 0:24].rearrange("p t (s e) -> p s t e", s=3)

            def col(k):
                return gv[:, k]

            hh = cp(col(0), gs.ap[:, 0, :].rearrange("p (t e) -> p t e", e=8), h, gfree)
            if top2:
                r = tt(flat, flat, gs.ap[:, 0, :], ALU.subtract, h)
                m1 = cp(gs.ap[:, 1, :], flat, r)
                cp(col(1), gs.ap[:, 1, :].rearrange("p (t e) -> p t e", e=8), m1)
                r = tt(flat, flat, gs.ap[:, 1, :], ALU.subtract, m1)
                hh = cp(col(2), lg, r)
            s.free = [hh]
            gs.free = [hh]
            bk = misc.next()
            for qt in range(4):
                m = tr(bk.ap[0:24, qt * P:(qt + 1) * P], gst[:, qt, :], hh, gz, bk.free, L["ident"])
            gfree[0] = m
            g = gT.next()
            c = cp(g.ap[0:24], bk.ap[0:24, :], m, g.free)
            bk.free = [c]
            return g, c

        def layer0():
            av = arena[:, :]
            qsb = av[:, 0:4096].rearrange("p (a c) -> p a c", a=8)
            kA = av[:, 4096:6144].rearrange("p (a c) -> p a c", a=4)
            kB = av[:, 6144:8192].rearrange("p (a c) -> p a c", a=4)
            vsb = av[:, 8192:9216].rearrange("p (t c) -> p t c", t=4)
            ysb = av[:, 9216:13312].rearrange("p (a c) -> p a c", a=8)
            qkv = av[:, 9216:15360].rearrange("p (b a c) -> p b a c", b=4, a=3)
            sc = av[:, 4096:9216].rearrange("p (a c) -> p a c", a=10)
            Sm = Ring([pbuf[:, i, 0, :].rearrange("p (a c) -> p a c", a=2) for i in range(4)])
            PTs = Ring([pbuf[:, i, 1, :] for i in range(4)])
            rq = Ring([sb(f"rq{i}", [P, 4, 16])[:, :, :] for i in range(2)])
            st2 = Ring([sb(f"st2{i}", [P, 8])[:, :] for i in range(3)])
            x1 = xn
            hn = res
            bS = Ring([A[0][:, 0, :], A[0][:, 1, :]])
            bT = Ring([A[1][:, 0, :], A[1][:, 1, :]])
            for r, src in ((bS, 0), (bT, 1)):
                for bf in r.bufs:
                    bf.free = pairs.bufs[src].free

            lnx = [lnorm(cols(xT, b), cols(xn, b), state["x"][b]) for b in range(NB)]
            lnh = [lnorm(cols(xn, b), cols(hn, b), lnx[b], w=vec("ln1w"), bb=vec("ln1b")) for b in range(NB)]
            ev = {}
            for b in range(NB):
                for k in range(3):
                    bk = misc.next()
                    m = mm(bk.ap, W["inp0"][:, k * P:(k + 1) * P], cols(hn, b), True, True, lnh[b], bk.free, L["inp0"])
                    ev[b, k] = act(qkv[:, b, k, :], bk.ap, ACT.Identity, m, bias=vec(f"inb{k}"))
                    bk.free = [ev[b, k]]
            ofree = []
            oW = {0: ev[0, 2]}
            oap = {0: qkv[:, 0, 2, :]}
            last_sc = None
            for s in range(1, NB):
                scs = []
                for t in range(s + 1):
                    tb = tF.next()
                    pr = tt(tb.ap, qkv[:, s, 0, :], qkv[:, t, 1, :], ALU.mult, ev[s, 0], ev[t, 1], tb.free, eng=PO)
                    bk = misc.next()
                    m = mm(bk.ap, W["blk8"][:, :], tb.ap, True, True, pr, bk.free, L["blk8"])
                    tb.free = [m]
                    c = act(sc[:, t, :], bk.ap, ACT.Copy, m, last_sc, scale=1.0 / math.sqrt(8.0))
                    bk.free = [c]
                    scs.append(c)
                mx = tt(sc[:, 4, :], sc[:, 0, :], sc[:, 1, :], ALU.max, scs)
                for t in range(2, s + 1):
                    mx = tt(sc[:, 4, :], sc[:, 4, :], sc[:, t, :], ALU.max, mx)
                exs = []
                for t in range(s + 1):
                    u = tt(sc[:, t, :], sc[:, t, :], sc[:, 4, :], ALU.subtract, mx)
                    exs.append(act(sc[:, t, :], sc[:, t, :], ACT.Exp, u))
                sm = tt(sc[:, 4, :], sc[:, 0, :], sc[:, 1, :], ALU.add, exs)
                for t in range(2, s + 1):
                    sm = tt(sc[:, 4, :], sc[:, 4, :], sc[:, t, :], ALU.add, sm)
                rc = rec(sc[:, 4, :], sc[:, 4, :], sm)
                pv = []
                for t in range(s + 1):
                    pv.append(tt(sc[:, t, :], sc[:, t, :], qkv[:, t, 2, :], ALU.mult, sm, ev[t, 2], eng=PO if t % 2 else DV))
                ac = pv[0]
                for t in range(1, s + 1):
                    ac = tt(sc[:, 0, :], sc[:, 0, :], sc[:, t, :], ALU.add, pv, ac)
                oap[s] = qkv[:, s, 0, :]
                oW[s] = tt(oap[s], sc[:, 0, :], sc[:, 4, :], ALU.mult, ac, rc)
                last_sc = oW[s]
            x1w = []
            for b in range(NB):
                bk = misc.next()
                m = mm(bk.ap, W["outp0"][:, :], oap[b], True, True, oW[b], bk.free, L["outp0"])
                x1b = qkv[:, b, 1, :]
                a = stt(x1b, bk.ap, vec("outb"), cols(xn, b), ALU.add, ALU.add, m, last_sc)
                bk.free = [a]
                c = tt(cols(xT, b), cols(xT, b), x1b, ALU.add, a, lnx[b])
                x1w.append((a, c))
            lnh2 = [lnorm(qkv[:, b, 1, :], cols(hn, b), x1w[b][0], w=vec("ln2w"), bb=vec("ln2b")) for b in range(NB)]
            kz = [fill(kA[64:128, :, :], 0.0, last_sc, eng=DV), fill(kB[0:64, :, :], 0.0, last_sc, eng=DV)]
            wk = tt(vec("wqk"), vec("qn"), vec("kn"), ALU.mult, L["vecs"])
            wk = ts(vec("wqk"), vec("wqk"), 0.125, None, ALU.mult, None, wk)
            attn_res = [None] * NB
            hist = {"q": [], "k": [], "v": [], "y": []}

            def attn(b):
                X = cols(xn, b)
                ssb = bankO
                qe = []
                for p in range(8):
                    bk = misc.next()
                    m = mm(bk.ap, W["wq0"][:, p * P:(p + 1) * P], X, True, True, lnx[b], bk.free, L["wq0"])
                    c = cp(qsb[:, p, :], bk.ap, m, hist["q"])
                    bk.free = [c]
                    qe.append(c)
                    s = tA.next()
                    sq = act(s.ap, qsb[:, p, :], ACT.Square, c, s.free)
                    j, i = p % 4, p // 4
                    ms = mm(ssb.ap[32 * j:32 * j + 32, :], W["ssel"][:, 32 * i:32 * i + 32], s.ap, i == 0, i == 1, sq,
                            ssb.free, L["ssel"])
                    s.free = [ms]
                    yield
                s = tA.next()
                e = ts(s.ap, ssb.ap, 1.0 / 64, 1e-6, ALU.mult, ALU.add, ms, s.free)
                ssb.free = [e]
                bk = misc.next()
                for t in range(4):
                    m = tr(bk.ap[:, t * P:(t + 1) * P], s.ap[:, t * P:(t + 1) * P], e, bk.free, L["ident"])
                s.free = [m]
                r = rq.next()
                c = cp(r.ap.rearrange("p t (j i) -> p t j i", i=4),
                       bk.ap.rearrange("p (t j i) -> p t j i", t=4, j=4)[:, :, :, 0:4], m, r.free)
                bk.free = [c]
                rqw = tt(r.ap.rearrange("p t j -> p (t j)"), r.ap.rearrange("p t j -> p (t j)"),
                         W["ohalf"][:, 0:64], ALU.pow, c, L["ohalf"], eng=PO)
                yield
                ke = []
                kts = []
                bs = misc.next()
                for kv in range(4):
                    bk = bT.next()
                    m = mm(bk.ap, W["wk0"][:, kv * P:(kv + 1) * P], X, True, True, lnx[b], bk.free, L["wk0"])
                    kt = tF.next()
                    c = cp(kt.ap, bk.ap, m, kt.free)
                    bk.free = [c]
                    s = tA.next()
                    sq = act(s.ap, kt.ap, ACT.Square, c, s.free)
                    for t in range(4):
                        m = mm(bs.ap[:, 4 * kv + t:4 * kv + t + 1], s.ap[:, t * P:(t + 1) * P], W["ssel"][:, 0:1], True, True,
                               sq, bs.free, L["ssel"])
                    s.free = [m]
                    kts.append(kt)
                st = small.next()
                e = ts(st.ap[:, 0:16], bs.ap[:, 0:16], 1.0 / 64, 1e-6, ALU.mult, ALU.add, m, st.free)
                bs.free = [e]
                pw = tt(st.ap[:, 16:32], st.ap[:, 0:16], W["ohalf"][:, 0:16], ALU.pow, e, L["ohalf"], eng=PO)
                for kv in range(4):
                    kt = kts[kv]
                    bk, m = spread([(st.ap[:, 16 + 4 * kv:20 + 4 * kv].unsqueeze(2), P)], tA, pw)
                    k1 = stt(kA[0:64, kv, :], kt.ap[0:64, :], vec("wqk")[0:64], bk.ap[0:64, :], ALU.mult, ALU.mult,
                             m, wk, hist["k"], kz)
                    k2 = stt(kB[64:128, kv, :], kt.ap[64:128, :], vec("wqk")[64:128], bk.ap[64:128, :], ALU.mult,
                             ALU.mult, m, wk, hist["k"], kz)
                    bk.free = [k2]
                    kt.free = [k2]
                    st.free = [m]
                    ke.append(k2)
                yield
                ve = []
                for t in range(4):
                    bk = misc.next()
                    m = mm(bk.ap[:, 0:256], X[:, t * P:(t + 1) * P], W["wv0"][:, :], True, True, lnx[b], bk.free, L["wv0"])
                    c = cp(vsb[:, t, :], bk.ap[:, 0:256], m, hist["v"])
                    bk.free = [c]
                    ve.append(c)
                    yield
                ye = []
                work = [(p, t) for p in range(8) for t in range(4)]
                front = {}
                back = {}

                def scores(p, t):
                    kv = p // 2
                    w = 128 if t == 0 else 256
                    k0 = 0 if t == 0 else (t - 1) * P
                    S = bS.next()
                    for hf, kk in ((0, kA), (1, kB)):
                        m = mm(S.ap[:, 256 * hf:256 * hf + w], qsb[:, p, t * P:(t + 1) * P], kk[:, kv, k0:k0 + w], True, True,
                               S.free, qe[p], ke[kv])
                    sm = Sm.next()
                    st = st2.next()
                    mo = 128 if t == 0 else 0
                    for hf in range(2):
                        a = op(DV, lambda e, hf=hf: e.tensor_tensor_reduce(
                            sm.ap[:, hf, 0:w], S.ap[:, 256 * hf:256 * hf + w], W["mband"][:, mo:mo + w], 1.0, -3e38,
                            ALU.add, ALU.max, st.ap[:, hf:hf + 1]), m, sm.free, st.free, L["mband"])
                    S.free = [a]
                    ix = (p % 4) * 4 + 2 * (p // 4)
                    nb = stt(st.ap[:, 2:4], st.ap[:, 0:2], -1.0, r.ap[:, t, ix:ix + 2], ALU.mult, ALU.mult, a, rqw)
                    for hf in range(2):
                        ex = act(sm.ap[:, hf, 0:w], sm.ap[:, hf, 0:w], ACT.Exp, nb, bias=st.ap[:, 2 + hf:3 + hf],
                                 scale=r.ap[:, t, ix + hf:ix + hf + 1], accum=st.ap[:, 4 + hf:5 + hf])
                    r.free = [ex]
                    rc = rec(st.ap[:, 6:8], st.ap[:, 4:6], ex)
                    for hf in range(2):
                        nm = ts(sm.ap[:, hf, 0:w], sm.ap[:, hf, 0:w], st.ap[:, 6 + hf:7 + hf], None, ALU.mult, None, rc, eng=PO)
                    st.free = [nm]
                    front[p, t] = (sm, nm, w)

                def turn(p, t):
                    sm, nm, w = front[p, t]
                    nblk = w // P
                    pt = bT.next()
                    for hf in range(2):
                        for k in range(nblk):
                            o = (hf * nblk + k) * P
                            m = tr(pt.ap[:, o:o + P], sm.ap[:, hf, k * P:(k + 1) * P], nm, pt.free, L["ident"])
                    sm.free = [m]
                    ps = PTs.next()
                    c = cp(ps.ap[:, 0:2 * w], pt.ap[:, 0:2 * w], m, ps.free) if t % 2 else \
                        act(ps.ap[:, 0:2 * w], pt.ap[:, 0:2 * w], ACT.Copy, m, ps.free)
                    pt.free = [c]
                    back[p, t] = (ps, c, nblk)

                def values(p, t):
                    ps, c, nblk = back[p, t]
                    kv = p // 2
                    for k in range(nblk):
                        for hf in range(2):
                            kb = t - nblk + 1 + k
                            o = (hf * nblk + k) * P
                            m = mm(bankO.ap[64 * hf:64 * hf + 64, t * P:(t + 1) * P], vsb[:, kb, kv * 64:kv * 64 + 64],
                                   ps.ap[:, o:o + P], k == 0, k == nblk - 1, c, ve, bankO.free if t == 0 else None)
                    ps.free = [m]
                    if t == 3:
                        yc = act(ysb[:, p, :], bankO.ap, ACT.Copy, m, hist["y"])
                        bankO.free = [yc]
                        ye.append(yc)
                    return m

                n = len(work)
                for i in range(n + 2):
                    if i < n:
                        scores(*work[i])
                    if 1 <= i <= n:
                        turn(*work[i - 1])
                    if i >= 2:
                        m = values(*work[i - 2])
                    yield
                hist["q"] = hist["k"] = hist["v"] = [m]
                bk = misc.next()
                for p in range(8):
                    m = mm(bk.ap, W["wo0"][:, p, :], ysb[:, p, :], p == 0, p == 7, ye[p], bk.free, L["wo0"])
                hist["y"] = [m]
                a = tt(cols(xT, b), cols(xT, b), bk.ap, ALU.add, m, x1w[b][1])
                bk.free = [a]
                attn_res[b] = a
                yield

            ffn_res = [None] * NB

            def ffn(b):
                H = cols(hn, b)
                g, gw = route(H, lnh2[b], "rt0", True)
                yield
                y = bankY
                for e in range(8):
                    gb = misc.next()
                    gm = mm(gb.ap, W["selE"][:, e, :], g.ap, True, True, gw, gb.free, L["selE"])
                    gs = tG.next()
                    gc = cp(gs.ap, gb.ap, gm, gs.free)
                    gb.free = [gc]
                    for f in range(2):
                        bk = misc.next()
                        m = mm(bk.ap, W["w1_0"][:, e, f * P:(f + 1) * P], H, True, True, lnh2[b], bk.free, L["w1_0"])
                        h = tH.next()
                        a = act(h.ap, bk.ap, ACT.Gelu, m, h.free)
                        bk.free = [a]
                        k = tt(h.ap, h.ap, gs.ap, ALU.mult, a, gc, eng=PO)
                        first, final = e == 0 and f == 0, e == 7 and f == 1
                        m = mm(y.ap, W["w2_0"][:, 2 * e + f, :], h.ap, first, final, k, y.free if first else None, L["w2_0"])
                        h.free = [m]
                    gs.free = [k]
                    yield
                g.free = [gm]
                ffn_res[b] = (y, m)
                yield

            for b in range(NB):
                interleave(attn(b), ffn(b), 0.2)
                y, m = ffn_res[b]
                a = tt(cols(xT, b), cols(xT, b), y.ap, ALU.add, m, attn_res[b])
                y.free = [a]
                state["x"][b] = [a]
            for r, src in ((bS, 0), (bT, 1)):
                pairs.bufs[src].free = [bf.free for bf in r.bufs]
            state["arena"] = [attn_res[NB - 1], a, Q.q[PE][-1]]

        def halves(src, parts_, w, free, rows):
            t = tF.next()
            h = cp(parts_[0:rows, 0, :], src, w, free)
            r1 = tt(t.ap[0:rows], src, parts_[0:rows, 0, :], ALU.subtract, h, t.free)
            m = cp(parts_[0:rows, 1, :], t.ap[0:rows], r1)
            r2 = tt(t.ap[0:rows], t.ap[0:rows], parts_[0:rows, 1, :], ALU.subtract, m)
            lo = cp(parts_[0:rows, 2, :], t.ap[0:rows], r2)
            t.free = [lo]
            return lo

        qpart, kpart, mpart = (w0[:, 768 * k:768 * (k + 1)].bitcast(BF16).rearrange("p (s c) -> p s c", s=3) for k in range(3))
        mxr = Ring([sb(f"mx{i}", [P, 4, 32])[:, :, :] for i in range(2)])
        ytok = w0[:, 2304:2816].rearrange("p (t c) -> p t c", t=4)
        yst = Ring([sb(f"yst{i}", [P, 4, 4])[:, :, :] for i in range(2)])
        pb = Ring([pbuf[:, i, :, :] for i in range(4)])
        free = {"qpart": [], "kpart": [], "mpart": [], "ytok": [], "res": []}

        class Heads:

            def __init__(self, lay, D, GK, kof, bufs, vbufs, causal, padded):
                self.lay, self.D, self.GK, self.kof, self.causal, self.padded = lay, D, GK, kof, causal, padded
                self.J = 16 // D
                self.G = 8 * self.J
                self.rows = 96 + 3 * self.J
                self.q = [v[:, 0:8 * T].rearrange("p (g c) -> p g c", c=T) for v in bufs]
                self.k = [v[:, 8 * T:(8 + GK) * T].rearrange("p (g c) -> p g c", c=T) for v in bufs]
                self.v = vbufs
                self.dr = {k: [nc.dram_tensor(f"scr{lay}{k}{b}", (3, r, T), BF16, kind="Internal").ap() for b in range(NB)]
                           for k, r in (("q", P), ("k", P), ("m", self.G))}
                self.ready = [None, None]
                self.used = [[], []]

            def clear(self, i, w):
                a = []
                if not self.padded:
                    a.append(fill(self.k[i].rearrange("p g c -> p (g c)").bitcast(F32), 0.0, w))
                n = f"kone{self.lay}"
                c = dma(f"{n}_{i}", self.k[i][96:self.rows, :, :], d[n].bitcast(BF16), w, a)
                z = fill(self.v[i], 0.0, w)
                o = op(DV, lambda e: e.memset(self.v[i][:, :, :, self.D:self.D + 1], 1.0), z)
                self.ready[i] = [a, c, z, o]

        def stack(H, b, qw, kw):
            i, D, lay = b % 2, H.D, H.lay
            w1 = dma(f"wq{lay}{b}", H.dr["q"][b].rearrange("s r c -> r s c"), qpart, qw)
            w2 = dma(f"wk{lay}{b}", H.dr["k"][b].rearrange("s r c -> r s c"), kpart, kw)
            free["qpart"], free["kpart"] = [w1], [w2]
            for n, (a, k) in enumerate(zip(QT, KT)):
                r = slice(16 * n, 16 * n + 16)
                lq = dma(f"sq{lay}{b}", H.q[i][r], H.dr["q"][b][PART[a]].rearrange("(r g) c -> r g c", g=8), w1, H.used[i], H.ready[i])
                ks = H.dr["k"][b][PART[k]].rearrange("(r g) c -> r g c", g=8)
                if H.padded:
                    lk = dma(f"sk{lay}{b}", H.k[i][r], ks, w2, H.used[i], H.ready[i])
                else:
                    for j in range(H.J):
                        lk = dma(f"sk{lay}{b}", H.k[i][16 * n + D * j:16 * n + D * j + D, 8 * j:8 * j + 8, :], ks[D * j:D * j + D],
                                 w2, H.used[i], H.ready[i])
            return [lq, lk]

        def maxima(H, b, st):
            i = b % 2
            mx = mxr.next()
            last_ = None
            for g in range(0, H.G, 2):
                if H.causal:
                    qr = []
                    for k in (0, 1):
                        p1 = pairs.next()
                        for t, o, bank in ((0, 0, 0), (2, P, 0), (1, 0, 1)):
                            n = (t + 1) * P
                            mm(p1.ap[:, bank, o:o + n], H.q[i][0:96, (g + k) % 8, t * P:(t + 1) * P], H.k[i][0:96, H.kof(g + k), 0:n],
                               True, False, p1.free, st, mx.free)
                            m = mm(p1.ap[:, bank, o + t * P:o + n], identb, mdiag, False, True, L["identb"], L["mdiag"])
                        for t, o, bank in ((0, 0, 0), (2, P, 0), (1, 0, 1)):
                            last_ = red(mx.ap[:, t, g + k:g + k + 1], p1.ap[:, bank, o:o + (t + 1) * P], ALU.max, m, mx.free)
                        p1.free = [last_]
                        yield None
                    p2 = pairs.next()
                    for k in (0, 1):
                        mm(p2.ap[:, k, :], H.q[i][0:96, (g + k) % 8, 3 * P:T], H.k[i][0:96, H.kof(g + k), :], True, False, p2.free, st)
                        m = mm(p2.ap[:, k, 3 * P:T], identb, mdiag, False, True, L["identb"], L["mdiag"])
                    last_ = red(mx.ap[:, 3, g:g + 2], p2.ap, ALU.max, m, mx.free)
                    p2.free = [last_]
                    yield None
                else:
                    for t in range(4):
                        p1 = pairs.next()
                        for k in (0, 1):
                            m = mm(p1.ap[:, k, :], H.q[i][0:96, (g + k) % 8, t * P:(t + 1) * P], H.k[i][0:96, H.kof(g + k), :],
                                   True, True, p1.free, st)
                        last_ = red(mx.ap[:, t, g:g + 2], p1.ap, ALU.max, m, mx.free)
                        p1.free = [last_]
                        yield None
            bk = misc.next()
            for t in range(4):
                m = tr(bk.ap[0:H.G, t * P:(t + 1) * P], mx.ap[:, t, 0:H.G], last_, bk.free, L["ident"])
            mx.free = [m]
            n_ = tF.next()
            ng = ts(n_.ap[0:H.G], bk.ap[0:H.G, :], -1.0, None, ALU.mult, None, m, n_.free)
            bk.free = [ng]
            lo = halves(n_.ap[0:H.G], mpart, ng, free["mpart"], H.G)
            n_.free = [lo]
            w1 = dma(f"wm{H.lay}{b}", H.dr["m"][b].rearrange("s r c -> r s c"), mpart[0:H.G, :, :], lo)
            free["mpart"] = [w1]
            l1 = dma(f"sm{H.lay}{b}", H.q[i][96:H.rows, :, :], H.dr["m"][b].rearrange("s (j g) c -> (s j) g c", g=8), w1)
            yield [l1]

        def weighted(H, b, tiles, st, ml, vw, put):
            i = b % 2
            steps = [(n, kb) for n in range(len(tiles)) for kb in range(4)]
            pend = None

            def flush(p):
                (n, kb), bufs, exs = p
                q0 = kb * P if H.causal else 0
                for j in range(4):
                    g, gv = tiles[n][j]
                    m = mm(bankO.ap[32 * j:32 * j + 32, q0:T], H.v[i][:, kb, gv, :], bufs[j // 2].ap[:, j % 2, 0:T - q0],
                           kb == 0, kb == 3, exs[j // 2], vw, bankO.free if kb == 0 else None)
                for bf in bufs:
                    bf.free = [m]
                if kb == 3:
                    o = tF.next()
                    oc = cp(o.ap, bankO.ap, m, o.free)
                    bankO.free = [oc]
                    bk = misc.next()
                    for t in range(4):
                        m2 = tr(bk.ap[:, t * P:(t + 1) * P], o.ap[:, t * P:(t + 1) * P], oc, bk.free, L["ident"])
                    o.free = [m2]
                    v = bk.ap.rearrange("p (t j r) -> p t j r", t=4, j=4)
                    s = yst.next()
                    rc = rec(s.ap, v[:, :, :, H.D], m2, s.free)
                    pw = put(n, v, s.ap, rc)
                    bk.free = [pw]
                    s.free = [pw]
                return m

            for n, kb in steps:
                q0 = kb * P if H.causal else 0
                bufs, exs = [], []
                for jj in range(2):
                    pr = pairs.next()
                    for k in range(2):
                        g, _ = tiles[n][2 * jj + k]
                        m = mm(pr.ap[:, k, 0:T - q0], H.k[i][0:H.rows, H.kof(g), kb * P:(kb + 1) * P],
                               H.q[i][0:H.rows, g % 8, q0:T],
                               True, not H.causal, pr.free, st, ml)
                        if H.causal:
                            m = mm(pr.ap[:, k, 0:P], identb, mdiagT, False, True, L["identb"], L["mdiagT"])
                    e = pb.next()
                    x = act(e.ap[:, :, 0:T - q0], pr.ap[:, :, 0:T - q0], ACT.Exp, m, e.free)
                    pr.free = [x]
                    bufs.append(e)
                    exs.append(x)
                if pend:
                    m = flush(pend)
                pend = ((n, kb), bufs, exs)
                yield
            m = flush(pend)
            H.used[i] = [m]
            yield

        identb, mdiag, mdiagT = W["identb"][:, :], W["mdiag"][:, :], W["mdiagT"][:, :]

        def project_out(b, w, waits, bias=None):
            bk = misc.next()
            for t in range(4):
                m = tr(bk.ap[:, t * P:(t + 1) * P], ytok[:, t, :], waits, bk.free, L["ident"])
            free["ytok"] = [m]
            y = tA.next()
            c = act(y.ap, bk.ap, ACT.Copy, m, y.free)
            bk.free = [c]
            bk = misc.next()
            m = mm(bk.ap, W[w][:, :], y.ap, True, True, c, bk.free, L[w])
            y.free = [m]
            if bias is None:
                a = tt(cols(xT, b), cols(xT, b), bk.ap, ALU.add, m)
            else:
                a = stt(cols(xT, b), bk.ap, vec(bias), cols(xT, b), ALU.add, ALU.add, m)
            bk.free = [a]
            return a

        def make1():
            a16 = arena[:, :].bitcast(BF16)
            bufs = [a16[:, 0:8192], a16[:, 8192:16384]]
            vb = [res[:, k * 1024:(k + 1) * 1024].rearrange("p (t g r) -> p t g r", t=4, g=8) for k in range(2)]
            H = Heads(1, 4, 8, lambda h: h % 8 // 4 * 4 + h // 8, bufs, vb, True, True)
            tU = Ring([sb(f"tU{k}", [P, T])[:, :] for k in range(2)])
            rs = sb("rs1", [P, 2, 80])
            a1 = w0[:, 2816:3328].rearrange("p (s t c) -> p s t c", s=2, t=4)
            S = {}
            ftk = {"rs": [], "a1": []}
            S["gain"] = ts(vec("gain"), vec("gain"), 0.5, None, ALU.mult, None, L["vecs"])

            def prep(b):
                if b < 2:
                    H.clear(b, S["start"])
                yield
                X = cols(xn, b)
                lw = lnorm(cols(xT, b), X, state["x"][b], state["xnfree"][b])
                S["ln", b] = lw
                yield
                rot, sqs = [], []
                for n in range(2):
                    o = 2 * n * P
                    bp = misc.next()
                    m = mm(bp.ap, W["wqk1"][:, o:o + P], X, True, True, lw, bp.free, L["wqk1"])
                    bs = misc.next()
                    m2 = mm(bs.ap, W["wqk1"][:, o + P:o + 2 * P], X, True, True, lw, bs.free)
                    u = tU.next()
                    u1 = tt(u.ap, bp.ap, W["cos1"][:, :], ALU.mult, m, u.free, L["cos1"])
                    s = tA.next()
                    sq = act(s.ap, bp.ap, ACT.Square, u1, s.free)
                    bp.free = [sq]
                    u2b = tF.next()
                    u2 = tt(u2b.ap, bs.ap, W["sin1"][:, :], ALU.mult, m2, u2b.free, L["sin1"])
                    bs.free = [u2]
                    u3 = tt(u.ap, u.ap, u2b.ap, ALU.add, u1, u2, eng=PO)
                    u2b.free = [u3]
                    rot.append((u, u3))
                    sqs.append((s, sq))
                    yield
                (u, u3), (k, k3) = rot
                (s, sq), (sk, sqk) = sqs
                bk = misc.next()
                for t in range(4):
                    mm(bk.ap[:, 20 * t:20 * t + 16], s.ap[:, t * P:(t + 1) * P], W["selq1"][:, :], True, True, sq, bk.free,
                       L["selq1"])
                    m = mm(bk.ap[:, 20 * t + 16:20 * t + 20], sk.ap[:, t * P:(t + 1) * P], W["selk1"][:, :], True, True,
                           sqk, L["selk1"])
                s.free = [m]
                sk.free = [m]
                e = ts(rs[:, 0, :], bk.ap[:, 0:80], float(np.finfo(np.float32).eps), None, ALU.add, None, m, ftk["rs"])
                bk.free = [e]
                r = tt(rs[:, 1, :], rs[:, 0, :], W["ohalf"][:, :], ALU.pow, e, L["ohalf"], eng=PO)
                yield
                bk = misc.next()
                for t in range(4):
                    m = mm(bk.ap[:, 64 * t:64 * t + 64], X[:, t * P:(t + 1) * P], W["wvg1"][:, :], True, True, lw, bk.free,
                           L["wvg1"])
                v4 = bk.ap[:, 0:256].rearrange("p (t s c) -> p t s c", t=4, s=2)
                tb = tF.next()
                th = act(tb.ap[:, 0:P].rearrange("p (t c) -> p t c", t=4), v4[:, :, 1, :], ACT.Tanh, m, tb.free, scale=0.5)
                g1 = stt(tb.ap[:, 0:P].rearrange("p (t c) -> p t c", t=4), tb.ap[:, 0:P].rearrange("p (t c) -> p t c", t=4),
                         1.0, v4[:, :, 0, :], ALU.add, ALU.mult, th)
                bk.free = [g1]
                vw = ts(H.v[b % 2][:, :, :, 0:4], tb.ap[:, 0:P].rearrange("p (t g i) -> p t g i", t=4, i=4), 0.5, None,
                        ALU.mult, None, g1, H.ready[b % 2], H.used[b % 2])
                tb.free = [vw]
                yield
                r3 = rs[:, 1, :].rearrange("p (t h) -> p t h", t=4)
                bk, m = spread([(r3[:, :, 4 * j:4 * j + 4], -8) for j in range(4)], tA, r)
                qw = stt(u.ap, u.ap, vec("gain"), bk.ap, ALU.mult, ALU.mult, m, u3, S["gain"])
                bk.free = [qw]
                qp = halves(u.ap, qpart, qw, free["qpart"], P)
                u.free = [qp]
                bk, m = spread([(r3[:, :, 16:20], 32)], tA, r)
                ftk["rs"] = [m]
                kw = tt(k.ap, k.ap, bk.ap, ALU.mult, m, k3)
                bk.free = [kw]
                kp = halves(k.ap, kpart, kw, free["kpart"], P)
                k.free = [kp]
                st = stack(H, b, qp, kp)
                yield
                ml = None
                for x in maxima(H, b, st):
                    ml = x
                    yield
                S["in", b] = (st, ml, vw)

            def main(b):
                st, ml, vw = S["in", b]
                tiles = [[(8 * j + 4 * hf + r, 2 * j + hf) for j in range(4)] for hf in range(2) for r in range(4)]
                ws = []

                def put(n, v, rinv, rc):
                    hf, r = n // 4, n % 4
                    dst = a1[:, hf, :, :].rearrange("p t (j r i) -> p t j r i", j=4, r=4)[:, :, :, r, :]
                    o = tt(dst, v[:, :, :, 0:4], rinv.unsqueeze(3).to_broadcast([P, 4, 4, 4]), ALU.mult, rc, ftk["a1"])
                    ws.append(o)
                    return o

                for _ in weighted(H, b, tiles, st, ml, vw, put):
                    yield
                lp = W["lp1"][:, :].unsqueeze(1).to_broadcast([P, 4, 64])
                a = tt(a1[:, 1, :, :], a1[:, 1, :, :], lp, ALU.mult, ws, L["lp1"])
                y8 = ytok[:, :, :].rearrange("p t (h s i) -> p t h s i", s=2, i=4)
                A1 = a1[:, 0, :, :].rearrange("p t (h i) -> p t h i", i=4)
                A2 = a1[:, 1, :, :].rearrange("p t (h i) -> p t h i", i=4)
                yw = []
                for t in range(4):
                    yw.append(tt(y8[:, t, :, 0, :], A1[:, t], A2[:, t], ALU.subtract, a, free["ytok"]))
                    yw.append(tt(y8[:, t, :, 1, :], A1[:, t], A2[:, t], ALU.add, a, free["ytok"]))
                ftk["a1"] = yw
                S["att", b] = project_out(b, "wo1", yw)
                yield

            def ffn(b):
                X = cols(xn, b)
                if b == 0:
                    W["dw1"] = wA[:, 0:3072].rearrange("p (e f) -> p e f", e=24)
                    L["dw1"] = dma("dw1", W["dw1"], d["dw1"], S["start"])
                    for k, n in enumerate(("gw1", "uw1")):
                        W[n] = arena[:, 8192 + 2816 * k:8192 + 2816 * (k + 1)]
                        L[n] = dma(n, W[n], d[n], S["start"])
                lw = S["ln", b]
                g, gw = route(X, lw, "rt1", True)
                yield
                y = bankY
                for e in range(8):
                    gb = misc.next()
                    gm = mm(gb.ap, W["selE"][:, e, :], g.ap, True, True, gw, gb.free, L["selE"])
                    xg = tG.next()
                    xw = stt(xg.ap, X, 0.5, gb.ap, ALU.mult, ALU.mult, gm, lw, xg.free)
                    gb.free = [xw]
                    for s, M in ((0, 128), (1, 128), (2, 96)):
                        o = e * 352 + s * P
                        bg = misc.next()
                        m1 = mm(bg.ap[0:M, :], W["gw1"][:, o:o + M], X, True, True, lw, bg.free, L["gw1"])
                        bu = misc.next()
                        m2 = mm(bu.ap[0:M, :], W["uw1"][:, o:o + M], xg.ap, True, True, xw, bu.free, L["uw1"])
                        h = tH.next()
                        th = act(h.ap[0:M], bg.ap[0:M, :], ACT.Tanh, m1, h.free, scale=0.5)
                        h1 = stt(h.ap[0:M], h.ap[0:M], 1.0, bg.ap[0:M, :], ALU.add, ALU.mult, th)
                        bg.free = [h1]
                        h2 = tt(h.ap[0:M], h.ap[0:M], bu.ap[0:M, :], ALU.mult, h1, m2)
                        bu.free = [h2]
                        first, final = e == 0 and s == 0, e == 7 and s == 2
                        m = mm(y.ap, W["dw1"][0:M, 3 * e + s, :], h.ap[0:M], first, final, h2, y.free if first else None,
                               L["dw1"])
                        h.free = [m]
                        yield
                    xg.free = [m2]
                g.free = [gm]
                S["ffn", b] = m

            def finish(b):
                a = tt(cols(xT, b), cols(xT, b), bankY.ap, ALU.add, S["ffn", b], S["att", b])
                bankY.free = [a]
                state["x"][b] = [a]
                state["xnfree"][b] = [S["ffn", b], a]

            return S, prep, main, ffn, finish

        def make2():
            a16 = arena[:, :].bitcast(BF16)
            bufs = [a16[:, 0:12288], a16[:, 12288:24576]]
            vb = [arena[:, 12288 + k * 2048:12288 + (k + 1) * 2048].rearrange("p (t g r) -> p t g r", t=4, g=16) for k in range(2)]
            H = Heads(2, 8, 16, lambda h: h, bufs, vb, False, False)
            S = {}

            def prep(b):
                if b < 2:
                    H.clear(b, S["start"])
                yield
                X = cols(xn, b)
                lw = lnorm(cols(xT, b), X, state["x"][b], state["xnfree"][b])
                S["ln", b] = lw
                yield
                pw = []
                for w, bias, part, sc in (("wq2", "bq2", qpart, 1.0 / math.sqrt(8.0)), ("wk2", "bk2", kpart, 1.0)):
                    bk = misc.next()
                    m = mm(bk.ap, W[w][:, :], X, True, True, lw, bk.free, L[w])
                    t = tF.next()
                    c = ts(t.ap, bk.ap, vec(bias), sc, ALU.add, ALU.mult, m, t.free, L["vecs"])
                    bk.free = [c]
                    pw.append(halves(t.ap, part, c, free["qpart" if w == "wq2" else "kpart"], P))
                    t.free = [pw[-1]]
                    yield
                st = stack(H, b, pw[0], pw[1])
                bk = misc.next()
                for t in range(4):
                    m = mm(bk.ap[:, t * P:(t + 1) * P], X[:, t * P:(t + 1) * P], W["wv2"][:, :], True, True, lw, bk.free, L["wv2"])
                vw = []
                for t in range(4):
                    vw.append(tt(H.v[b % 2][:, t, :, 0:8], bk.ap[:, t * P:(t + 1) * P].rearrange("p (h i) -> p h i", i=8),
                                 W["bv2"][:, :].rearrange("p (h i) -> p h i", i=8), ALU.add, m, L["bv2"],
                                 H.ready[b % 2], H.used[b % 2]))
                bk.free = vw
                yield
                ml = None
                for x in maxima(H, b, st):
                    ml = x
                    yield
                S["in", b] = (st, ml, vw)

            def main(b):
                st, ml, vw = S["in", b]
                tiles = [[(4 * r + j, 4 * r + j) for j in range(4)] for r in range(4)]
                ws = []

                def put(n, v, rinv, rc):
                    dst = ytok[:, :, :].rearrange("p t (n j i) -> p t n j i", n=4, i=8)[:, :, n, :, :]
                    o = tt(dst, v[:, :, :, 0:8], rinv.unsqueeze(3).to_broadcast([P, 4, 4, 8]), ALU.mult, rc, free["ytok"])
                    ws.append(o)
                    return o

                for _ in weighted(H, b, tiles, st, ml, vw, put):
                    yield
                S["att", b] = project_out(b, "wo2", ws, "bo2")
                yield

            def ffn(b):
                X = cols(xn, b)
                lw = S["ln", b]
                g, gw = route(X, lw, "rt2", False, "rb2")
                yield
                bk = misc.next()
                m = mm(bk.ap[0:64, :], W["la2"][:, :], X, True, True, lw, bk.free, L["la2"])
                z = tH.next()
                c = act(z.ap[0:64], bk.ap[0:64, :], ACT.Copy, m, z.free, scale=2.0)
                bk.free = [c]
                bk = misc.next()
                m = mm(bk.ap[0:64, :], W["selR"][:, :], g.ap, True, True, gw, bk.free, L["selR"])
                g.free = [m]
                c = tt(z.ap[0:64], z.ap[0:64], bk.ap[0:64, :], ALU.mult, m, c)
                bk.free = [c]
                y = bankY
                mm(y.ap, W["base2"][:, :], X, True, False, lw, y.free, L["base2"])
                m = mm(y.ap, W["lb2"][:, :], z.ap[0:64], False, True, c, L["lb2"])
                z.free = [m]
                S["ffn", b] = m
                yield

            def finish(b):
                a = stt(cols(xT, b), bankY.ap, vec("bb2"), cols(xT, b), ALU.add, ALU.add, S["ffn", b], S["att", b])
                bankY.free = [a]
                state["x"][b] = [a]
                state["xnfree"][b] = [S["ffn", b], a]

            return S, prep, main, ffn, finish

        def make3():
            S = {}
            tok = arena[:, 0:1536].rearrange("p (t s c) -> p t s c", t=4, s=3)
            s3 = arena[:, 1536:2048].rearrange("p (s c) -> p s c", s=8)
            c3 = sb("c3", [P, 6, 16])
            kvm = sb("kvm", [P, P])
            fr = {"tok": state["arena"], "s3": state["arena"]}
            EPS = 1e-6

            def prep(b):
                if b == 0:
                    wi = res[:, 0:1152].bitcast(I32)
                    li = dma("wi3", wi, d["wi3"], S["start"])
                    S["deq"] = ts(wA[:, 0:1152], wi, 1.0 / 127.0, None, ALU.mult, None, li, S["start"])
                yield
                X = cols(xn, b)
                S["ln", b] = lnorm(cols(xT, b), X, state["x"][b], state["xnfree"][b])
                yield

            def main(b):
                X = cols(xn, b)
                lw = S["ln", b]
                d_, dw = {}, {}
                for n, (w, bias) in enumerate((("wq3", "bq3"), ("wk3", "bk3"))):
                    bk = misc.next()
                    m = mm(bk.ap, W[w][:, :], X, True, True, lw, bk.free, L[w])
                    t = tF.next()
                    hb = S.get("hb" + bias)
                    if hb is None:
                        hb = S["hb" + bias] = ts(vec(bias), vec(bias), 0.5, None, ALU.mult, None, L["vecs"])
                    a = act(t.ap, bk.ap, ACT.Tanh, m, hb, t.free, bias=vec(bias), scale=0.5)
                    bk.free = [a]
                    dw[n] = op(DV, lambda e, t=t, n=n: e.tensor_scalar(t.ap, t.ap, 1.0, 0.5, ALU.add, ALU.mult), a)
                    d_[n] = t
                    sm = red(c3[:, 0, n:n + 1], t.ap, ALU.add, dw[n], fr["s3"])
                    dw["s", n] = ts(c3[:, 0, n:n + 1], c3[:, 0, n:n + 1], EPS, None, ALU.add, None, sm)
                    bk = misc.next()
                    for q in range(4):
                        m = tr(bk.ap[:, q * P:(q + 1) * P], t.ap[:, q * P:(q + 1) * P], dw[n], bk.free, L["ident"])
                    dw["t", n] = cp(tok[:, :, n, :], bk.ap.rearrange("p (t c) -> p t c", t=4), m, fr["tok"])
                    bk.free = [dw["t", n]]
                    te = tG.next()
                    dw["e", n] = ts(te.ap, t.ap, EPS, None, ALU.add, None, dw[n], te.free)
                    d_["e", n] = te
                    yield
                bk = misc.next()
                for q in range(4):
                    m = mm(bk.ap[:, q * P:(q + 1) * P], X[:, q * P:(q + 1) * P], W["wv3"][:, :], True, True, lw, bk.free, L["wv3"])
                vw = tt(tok[:, :, 2, :], bk.ap.rearrange("p (t c) -> p t c", t=4),
                        W["bv3"][:, :].unsqueeze(1).to_broadcast([P, 4, P]), ALU.add, m, L["bv3"], fr["tok"])
                bk.free = [vw]

                def dots(n, colsel, w, dst, f):
                    c = ts(c3[:, colsel, :], W["hsel"][:, :], c3[:, 0, n_of[colsel]:n_of[colsel] + 1], None, ALU.mult, None, w,
                           L["hsel"]) if colsel < 3 else w
                    bk = misc.next()
                    for q in range(4):
                        m = mm(bk.ap[:, 16 * q:16 * q + 16], d_["e", n].ap[:, q * P:(q + 1) * P], c3[:, colsel, :], True, True,
                               c, dw["e", n], bk.free)
                    o = f(dst, bk.ap[:, 0:64], m)
                    bk.free = [o]
                    return o

                n_of = {1: 1, 2: 0}
                si, so, cs, ce = s3[:, 0, :], s3[:, 1, :], s3[:, 2, :], s3[:, 3, :]
                w_si = dots(0, 1, dw["s", 1], si, lambda o, i_, m: rec(o, i_, m, fr["s3"]))
                w_so = dots(1, 2, dw["s", 0], so, lambda o, i_, m: rec(o, i_, m, fr["s3"]))
                yield
                w = {}
                for col_, n, st, ws in ((3, 1, so, w_so), (4, 0, si, w_si)):
                    bk = misc.next()
                    for q in range(4):
                        m = mm(bk.ap[:, 0:16], tok[:, q, n, :], st[:, 16 * q:16 * q + 16], q == 0, q == 3, ws, dw["t", n], bk.free)
                    a = ts(c3[:, col_, :], bk.ap[:, 0:16], EPS, None, ALU.add, None, m)
                    bk.free = [a]
                    w[col_] = tt(c3[:, col_, :], c3[:, col_, :], W["hsel"][:, :], ALU.mult, a, L["hsel"])
                w_cs = dots(0, 3, w[3], cs, lambda o, i_, m: act(o, i_, ACT.Exp, m, fr["s3"], scale=-1.0))
                w_ce = dots(1, 4, w[4], ce, lambda o, i_, m: ts(o, i_, -1.0, 1.0, ALU.max, ALU.min, m, fr["s3"]))
                w_cs = ts(cs, cs, 1.0, None, ALU.add, None, w_cs)
                w_cs = rec(cs, cs, w_cs)
                w_cs = tt(cs, cs, si, ALU.mult, w_cs, w_si)
                w_ce = act(ce, ce, ACT.Exp, w_ce)
                bk = misc.next()
                m = mm(bk.ap[:, 0:64], W["ones"][:, :], ce, True, True, w_ce, bk.free, L["ones"])
                a = red(c3[:, 5, :], bk.ap[:, 0:64].rearrange("p (t h) -> p h t", t=4), ALU.add, m)
                bk.free = [a]
                a = rec(c3[:, 5, :], c3[:, 5, :], a)
                a = ts(c3[:, 5, :], c3[:, 5, :], float(T) / P, None, ALU.mult, None, a)
                sc = s3[:, 4, :]
                w_sc = tt(sc.rearrange("p (t h) -> p t h", t=4), ce.rearrange("p (t h) -> p t h", t=4),
                          c3[:, 5, :].unsqueeze(1).to_broadcast([P, 4, 16]), ALU.mult, a, w_ce)
                yield
                vs = []
                for q in range(4):
                    v3 = tok[:, q, 2, :].rearrange("p (h i) -> p h i", i=8)
                    vs.append(tt(v3, v3, sc[:, 16 * q:16 * q + 16].unsqueeze(2).to_broadcast([P, 16, 8]), ALU.mult, w_sc, vw))
                bk = misc.next()
                for q in range(4):
                    m = mm(bk.ap[:, 0:P], tok[:, q, 1, :], tok[:, q, 2, :], q == 0, q == 3, vs, dw["t", 1], bk.free)
                kw = tt(kvm[:, :], bk.ap[:, 0:P], W["blk8"][:, :], ALU.mult, m, L["blk8"])
                bk.free = [kw]
                fr["tok"] = [m]
                bk = misc.next()
                for q in range(4):
                    m = mm(bk.ap[:, q * P:(q + 1) * P], d_[0].ap[:, q * P:(q + 1) * P], kvm[:, :], True, True, kw, bk.free)
                ys = []
                for q in range(4):
                    ys.append(tt(ytok[:, q, :].rearrange("p (h i) -> p h i", i=8),
                                 bk.ap[:, q * P:(q + 1) * P].rearrange("p (h i) -> p h i", i=8),
                                 cs[:, 16 * q:16 * q + 16].unsqueeze(2).to_broadcast([P, 16, 8]), ALU.mult, m, w_cs, free["ytok"]))
                bk.free = ys
                fr["s3"] = [ys[-1], m]
                for k in (0, 1, ("e", 0), ("e", 1)):
                    d_[k].free = [m]
                yield
                S["att", b] = project_out(b, "wo3", ys, "bo3")
                yield

            def ffn(b):
                X = cols(xn, b)
                lw = S["ln", b]
                wg, wu, wd = wA[:, 0:384], wA[:, 384:768], wA[:, 768:1152]
                y = bankY
                for s in range(3):
                    bg = misc.next()
                    m1 = mm(bg.ap, wg[:, s * P:(s + 1) * P], X, True, True, lw, bg.free, S["deq"])
                    bu = misc.next()
                    m2 = mm(bu.ap, wu[:, s * P:(s + 1) * P], X, True, True, lw, bu.free)
                    h = tH.next()
                    th = act(h.ap, bg.ap, ACT.Tanh, m1, h.free, scale=0.5)
                    h1 = stt(h.ap, h.ap, 1.0, bg.ap, ALU.add, ALU.mult, th)
                    bg.free = [h1]
                    h2 = stt(h.ap, h.ap, 0.5, bu.ap, ALU.mult, ALU.mult, h1, m2)
                    bu.free = [h2]
                    m = mm(y.ap, wd[:, s * P:(s + 1) * P], h.ap, s == 0, s == 2, h2, y.free if s == 0 else None)
                    h.free = [m]
                    yield
                S["ffn", b] = m

            def finish(b):
                a = tt(cols(xT, b), cols(xT, b), bankY.ap, ALU.add, S["ffn", b], S["att", b])
                bankY.free = [a]
                state["x"][b] = [a]
                state["xnfree"][b] = [S["ffn", b], a]

            return S, prep, main, ffn, finish

        state["xnfree"] = [[] for _ in range(NB)]
        state["arena"] = []
        if 0 in layers:
            layer0()
        for k in free:
            free[k] = list(state["arena"])
        stages = []
        for lay, make, ratio in ((1, make1, 1.0), (2, make2, 0.5), (3, make3, 1.0)):
            if lay in layers:
                made = make()
                stages += [(lay, b, made, ratio) for b in range(NB)]

        def chain(*gens):
            for g in gens:
                yield from g

        def begin(n):
            lay, b, (S, prep, _, _, _), _ = stages[n]
            if b == 0:
                S["start"] = state["arena"] if lay != 2 or 1 not in layers else [state["x"][3]]
            return prep(b)

        for n, (lay, b, (S, prep, main, ffn, finish), ratio) in enumerate(stages):
            if n == 0 or b == 0:
                for _ in begin(n):
                    pass
            nxt = stages[n + 1] if n + 1 < len(stages) and stages[n + 1][1] > 0 else None
            side = chain(begin(n + 1), ffn(b)) if nxt else ffn(b)
            interleave(main(b), side, 1.5)
            finish(b)
            state["arena"] = [state["x"][b], Q.q[PE][-1]]

        for b in range(NB):
            fin = dma("out", out[:, b * T:(b + 1) * T], cols(xT, b), state["x"][b])
        op(SY, lambda e: e.nop(), fin)
        Q.emit()


VECS = ["ln1w", "ln1b", "ln2w", "ln2b", "inb0", "inb1", "inb2", "outb", "qn", "kn", "wqk",
        "gain", "bq2", "bk2", "bo2", "bb2", "bq3", "bk3", "bo3"]


def constants():
    c = {}

    def bf(a):
        return (np.ascontiguousarray(a, dtype=np.float32).view(np.uint32) >> 16).astype(np.uint16)

    i = np.arange(P)
    c["ident"] = np.eye(P, dtype=np.float32)
    c["identb"] = bf(np.eye(P))
    c["ones"] = np.full((P, P), 1.0 / P, np.float32)
    c["ohalf"] = np.full((P, 80), -0.5, np.float32)
    c["blk8"] = (i[:, None] // 8 == i[None] // 8).astype(np.float32)
    j = np.arange(256)
    dist = i[:, None] + P - j[None]
    c["mband"] = np.where((dist >= 0) & (dist < 64), 0.0, NEG).astype(np.float32)
    c["mdiag"] = bf(np.where(i[None] <= i[:, None], 0.0, NEG))
    c["mdiagT"] = bf(np.where(i[:, None] <= i[None], 0.0, NEG))
    sel = np.zeros((P, 8, P), np.float32)
    for e in range(8):
        sel[[e, 8 + e, 16 + e], e, :] = 1
    c["selE"] = bf(sel)
    s = np.zeros((P, 64), np.float32)
    for e in range(8):
        s[e, 8 * e:8 * e + 8] = 1
    c["selR"] = bf(s)
    ss = np.zeros((P, 2, 32), np.float32)
    for k in range(2):
        ss[0:64, k, 2 * k] = 1
        ss[64:128, k, 2 * k + 1] = 1
    c["ssel"] = ss.reshape(P, 64)
    tl = (np.arange(8)[None] < np.arange(8)[:, None]).astype(np.float32)
    c["tril8"] = np.ascontiguousarray(np.broadcast_to(np.tile(tl, (4, 1))[None], (P, 32, 8)))
    pi = i // 8 % 4
    ang = (np.arange(0, 8, 2, dtype=np.float32) / np.float32(8) * np.float32(math.pi)).astype(np.float32)
    pos = np.arange(T, dtype=np.float32)
    rad = (np.float32(1) / (np.float32(1) + pos * np.float32(0.01))).astype(np.float32)
    a = (pos[:, None] * ang[None]).astype(np.float32)
    co = (rad[:, None] * np.cos(a)).astype(np.float32).T
    si = (rad[:, None] * np.sin(a)).astype(np.float32).T
    c["cos1"] = np.ascontiguousarray(co[pi])
    c["sin1"] = np.ascontiguousarray(np.where((i % 8 < 4)[:, None], si[pi], -si[pi]))
    c["selq1"] = ((i // 32 * 4 + i % 4)[:, None] == np.arange(16)[None]) * np.float32(1 / 8)
    c["selk1"] = ((i // 32)[:, None] == np.arange(4)[None]) * np.float32(1 / 8)
    c["selq1"], c["selk1"] = c["selq1"].astype(np.float32), c["selk1"].astype(np.float32)
    one = np.zeros((3, 4, 8, T), np.float32)
    for h in range(8):
        one[:, h % 4, h] = 1
    c["kone1"] = bf(one.reshape(12, 8, T))
    one = np.zeros((3, 2, 16, T), np.float32)
    for h in range(16):
        one[:, h // 8, h] = 1
    c["kone2"] = bf(one.reshape(6, 16, T))
    c["hsel"] = (i[:, None] // 8 == np.arange(16)[None]).astype(np.float32)
    return c


def layout(x):
    f = {}

    def T_(a):
        return np.ascontiguousarray(np.asarray(a).T)

    f["xT"] = T_(np.asarray(x["L0_attn_x"]).reshape(NT, P))
    f["wq0"] = T_(x["L0_attn_wq"])
    k = np.asarray(x["L0_attn_wk"]).reshape(4, 1, 64, P)
    f["wk0"] = T_(np.concatenate([k, k], 1).reshape(512, P))
    f["wv0"] = T_(x["L0_attn_wv"])
    f["wo0"] = np.ascontiguousarray(np.asarray(x["L0_attn_wo"]).T.reshape(8, P, P).transpose(1, 0, 2))
    f["inp0"] = T_(x["L0_ffn_in_proj_w"])
    f["outp0"] = T_(x["L0_ffn_out_proj_w"])
    f["rt0"] = T_(x["L0_ffn_router_w"])
    f["w1_0"] = np.ascontiguousarray(np.asarray(x["L0_ffn_w1"]).transpose(1, 0, 2))
    f["w2_0"] = np.ascontiguousarray(np.asarray(x["L0_ffn_w2"]).reshape(16, P, P).transpose(1, 0, 2))
    v = np.zeros((P, len(VECS)), np.float32)

    def put(n, a):
        v[:, VECS.index(n)] = np.asarray(a)

    put("ln1w", x["L0_ffn_ln1_w"])
    put("ln1b", x["L0_ffn_ln1_b"])
    put("ln2w", x["L0_ffn_ln2_w"])
    put("ln2b", x["L0_ffn_ln2_b"])
    for k in range(3):
        put(f"inb{k}", np.asarray(x["L0_ffn_in_proj_b"])[k * P:(k + 1) * P])
    put("outb", x["L0_ffn_out_proj_b"])
    put("qn", np.tile(np.asarray(x["L0_attn_q_norm_w"]), 2))
    put("kn", np.tile(np.asarray(x["L0_attn_k_norm_w"]), 2))
    put("gain", np.broadcast_to(np.asarray(x["L1_attn_q_gain"]).reshape(4, 1, 1, 4), (4, 4, 2, 4)).reshape(P))
    o2 = np.arange(P).reshape(2, 8, 8).transpose(0, 2, 1).reshape(P)
    put("bq2", np.asarray(x["L2_attn_bq"])[o2])
    put("bk2", np.asarray(x["L2_attn_bk"])[o2])
    f["wq2"] = T_(np.asarray(x["L2_attn_Wq"])[o2])
    f["wk2"] = T_(np.asarray(x["L2_attn_Wk"])[o2])
    for n, s in (("bo2", "L2_attn_bo"), ("bb2", "L2_ffn_base_b"),
                 ("bq3", "L3_attn_bq"), ("bk3", "L3_attn_bk"), ("bo3", "L3_attn_bo")):
        put(n, x[s])
    f["vecs"] = v

    def rep(a):
        return np.ascontiguousarray(np.broadcast_to(np.asarray(a).reshape(1, -1), (P, np.asarray(a).size)))

    wq = np.asarray(x["L1_attn_Wq"]).reshape(4, 4, 2, 4, P).transpose(0, 3, 2, 1, 4)
    wk = np.zeros((4, 4, 2, 4, P), np.float32)
    for j in range(4):
        wk[j, :, :, j] = np.asarray(x["L1_attn_Wk"]).reshape(4, 2, 4, P)[j].transpose(1, 0, 2)
    f["wqk1"] = T_(np.concatenate([w.reshape(P, P) for w in (wq, wq[:, :, ::-1], wk, wk[:, :, ::-1])]))
    f["wvg1"] = T_(np.concatenate([np.asarray(x["L1_attn_Wv"]), np.asarray(x["L1_attn_Wg"])]))
    f["wo1"] = T_(x["L1_attn_Wo"])
    f["lp1"] = rep(np.repeat(np.asarray(x["L1_attn_lambda_param"]), 4))
    f["rt1"] = T_(x["L1_ffn_router_w"])
    f["gw1"] = T_(np.asarray(x["L1_ffn_gate_w"]).reshape(-1, P))
    f["uw1"] = T_(np.asarray(x["L1_ffn_up_w"]).reshape(-1, P))
    dw = np.zeros((8, 384, P), np.float32)
    dw[:, 0:352] = np.asarray(x["L1_ffn_down_w"]).transpose(0, 2, 1)
    f["dw1"] = np.ascontiguousarray(dw.reshape(24, P, P).transpose(1, 0, 2))
    for n, s in (("wv2", "L2_attn_Wv"), ("wo2", "L2_attn_Wo"),
                 ("base2", "L2_ffn_base_w"), ("rt2", "L2_ffn_router_w"),
                 ("wq3", "L3_attn_Wq"), ("wk3", "L3_attn_Wk"), ("wv3", "L3_attn_Wv"), ("wo3", "L3_attn_Wo")):
        f[n] = T_(x[s])
    f["bv2"] = rep(x["L2_attn_bv"])
    f["bv3"] = rep(x["L3_attn_bv"])
    f["rb2"] = rep(x["L2_ffn_router_b"])
    f["la2"] = np.ascontiguousarray(np.tile(np.asarray(x["L2_ffn_lora_A"]), (1, 8)))
    f["lb2"] = np.ascontiguousarray(np.asarray(x["L2_ffn_lora_B"]).reshape(64, P))
    wd = np.asarray(x["L3_ffn_w_down"]).T.reshape(3, P, P).transpose(1, 0, 2).reshape(P, 384)
    f["wi3"] = np.ascontiguousarray(np.concatenate([np.asarray(x["L3_ffn_w_gate"]).T, np.asarray(x["L3_ffn_w_up"]).T, wd], 1))
    return f


def kernel(_layers=(0, 1, 2, 3), **inputs):
    import concourse.bacc as bacc
    from concourse.bass_utils import run_bass_kernel_spmd as run

    nc = bacc.Bacc("TRN2", target_bir_lowering=False, num_devices=1)
    arrays = {**constants(), **layout(inputs)}
    d = {n: nc.dram_tensor("in_" + n, a.shape, mybir.dt.from_np(a.dtype), kind="ExternalInput").ap()
         for n, a in arrays.items()}
    out = nc.dram_tensor("out_x", (P, NT), F32, kind="ExternalOutput").ap()
    build(nc, d, out, _layers)
    r = run(nc, [{"in_" + n: a for n, a in arrays.items()}], core_ids=[0])
    return np.ascontiguousarray(np.asarray(r.results[0]["out_x"]).T).reshape(NB, T, P)
```

```python
import math
from contextlib import ExitStack

import numpy as np
import concourse.bass as bass
from concourse import mybir

F32 = mybir.dt.float32
BF16 = mybir.dt.bfloat16
I32 = mybir.dt.int32
ALU = mybir.AluOpType
ACT = mybir.ActivationFunctionType
AX = mybir.AxisListType

P = 128
NB = 4
T = 512
NT = NB * T
NEG = -1e30
PE, AC, DV, PO, SY = "tensor", "scalar", "vector", "gpsimd", "sync"
QT = ("h", "h", "m", "m", "h", "l")
KT = ("h", "m", "h", "m", "l", "h")
PART = {"h": 0, "m": 1, "l": 2}


class Op:

    def __init__(self, eng, fn, waits):
        self.eng, self.fn, self.waits = eng, fn, waits
        self.flag, self.sem, self.val = False, None, 0


class Landed:

    def __init__(self, sem, val):
        self.sem, self.val = sem, val


class Queues:

    def __init__(self, nc, ctx):
        self.nc, self.ctx = nc, ctx
        self.q = {e: [] for e in (PE, AC, DV, PO, SY)}
        self.sem = {e: ctx.enter_context(nc.semaphore("done_" + e)) for e in (PE, AC, DV, PO)}
        self.dma_sems = {}

    def op(self, eng, fn, *waits):
        flat = []

        def add(w):
            if w is None:
                return
            if isinstance(w, (list, tuple)):
                for x in w:
                    add(x)
                return
            if isinstance(w, Op):
                w.flag = True
            flat.append(w)

        add(waits)
        o = Op(eng, fn, flat)
        self.q[eng].append(o)
        return o

    def dma(self, name, out, in_, *waits, eng=SY):
        if name not in self.dma_sems:
            self.dma_sems[name] = [self.ctx.enter_context(self.nc.semaphore("dma_" + name)), 0]
        s = self.dma_sems[name]
        s[1] += 16
        o = self.op(eng, lambda e: e.dma_start(out, in_), *waits)
        o.sem = s[0]
        return Landed(s[0], s[1])

    def emit(self):
        for e in (PE, AC, DV, PO):
            n = 0
            for o in self.q[e]:
                if o.flag and o.sem is None:
                    n += 1
                    o.val = n
        block = self.ctx.enter_context(self.nc.Block())
        for name in (SY, PE, AC, DV, PO):
            def body(eng, name=name):
                seen = {}
                for o in self.q[name]:
                    need = {}
                    for w in o.waits:
                        s = w.sem if isinstance(w, Landed) else self.sem[w.eng]
                        need[id(s)] = (s, max(w.val, need.get(id(s), (s, 0))[1]))
                    for k, (s, v) in need.items():
                        if seen.get(k, 0) < v:
                            eng.wait_ge(s, v)
                            seen[k] = v
                    ins = o.fn(eng)
                    if o.sem is not None:
                        ins.then_inc(o.sem, 16)
                    elif o.flag:
                        ins.then_inc(self.sem[name], 1)
            blocks = {SY: block.sync, PE: block.tensor, AC: block.scalar, DV: block.vector, PO: block.gpsimd}
            blocks[name](body)


class Buf:

    def __init__(self, ap):
        self.ap, self.busy, self._free = ap, False, []

    @property
    def free(self):
        return self._free

    @free.setter
    def free(self, readers):
        self._free, self.busy = readers, False


class Ring:
    def __init__(self, aps):
        self.bufs, self.n = [Buf(a) for a in aps], 0

    def next(self):
        b = self.bufs[self.n % len(self.bufs)]
        self.n += 1
        assert not b.busy, "a buffer is taken before its last use is queued"
        b.busy = True
        return b


def build(nc, d, out, layers=(0, 1, 2, 3), parts=("attn", "ffn"), last="x"):
    ctx = ExitStack()
    with ctx:
        Q = Queues(nc, ctx)
        op, dma = Q.op, Q.dma

        def sb(name, shape, dt=F32):
            return ctx.enter_context(nc.sbuf_tensor(name, shape, dt))

        A = [ctx.enter_context(nc.psum_tensor(f"psA{i}", [P, 2, T], F32)) for i in range(2)]
        B = [ctx.enter_context(nc.psum_tensor(f"psB{i}", [P, T], F32)) for i in range(4)]
        pairs = Ring([a[:, :, :] for a in A])
        bankO = Buf(B[0][:, :])
        misc = Ring([B[1][:, :], B[2][:, :]])
        bankY = Buf(B[3][:, :])

        def mm(out, lhsT, rhs, start, stop, *waits):
            return op(PE, lambda e: e.matmul(out, lhsT, rhs, start=start, stop=stop, skip_group_check=True), *waits)

        def tr(out, in_, *waits):
            return op(PE, lambda e: e.transpose(out, in_, ident[0:in_.shape[0], 0:in_.shape[0]]), *waits)

        def act(out, in_, f, *waits, bias=0.0, scale=1.0, accum=None):
            kw = {} if accum is None else {"accum_out": accum}
            if f == ACT.Copy and bias == 0.0:
                return op(AC, lambda e: e.activation(out, in_, f, scale=scale, **kw), *waits)
            return op(AC, lambda e: e.activation(out, in_, f, bias=bias, scale=scale, **kw), *waits)

        def tt(out, a, b, o, *waits, eng=DV):
            return op(eng, lambda e: e.tensor_tensor(out, a, b, o), *waits)

        def ts(out, a, s1, s2, o1, o2, *waits, eng=DV):
            if s2 is None:
                return op(eng, lambda e: e.tensor_scalar(out, a, s1, None, o1), *waits)
            return op(eng, lambda e: e.tensor_scalar(out, a, s1, s2, o1, o2), *waits)

        def stt(out, a, s, b, o1, o2, *waits):
            return op(DV, lambda e: e.scalar_tensor_tensor(out, a, s, b, o1, o2), *waits)

        def cp(out, a, *waits, eng=DV):
            return op(eng, lambda e: e.tensor_copy(out, a), *waits)

        def red(out, a, o, *waits):
            return op(DV, lambda e: e.tensor_reduce(out, a, AX.X, o), *waits)

        def rec(out, a, *waits):
            return op(DV, lambda e: e.reciprocal(out, a), *waits)

        def fill(out, v, *waits, eng=PO):
            return op(eng, lambda e: e.memset(out, v), *waits)

        W = {}
        L = {}
        wA = sb("wA", [P, 4096])
        w0 = sb("w0", [P, 3328])
        arena = sb("arena", [P, 17920])

        def load(name, dt=F32):
            h = d[name]
            W[name] = sb("w_" + name, list(h.shape), dt)
            full = tuple(slice(None) for _ in h.shape)
            L[name] = dma(name, W[name][full], h.bitcast(BF16) if dt == BF16 else h)

        xT = sb("xT", [P, NT])
        Lx = [dma(f"x{b}", xT[:, b * T:(b + 1) * T], d["xT"][:, b * T:(b + 1) * T]) for b in range(NB)]
        for n in ("ident", "ones", "blk8", "mband", "vecs", "hsel"):
            load(n)
        for n in ("identb", "mdiagT", "selE", "selR"):
            load(n, BF16)
        ident = W["ident"]
        vecs = W["vecs"]
        VEC = {n: i for i, n in enumerate(VECS)}

        def vec(n):
            i = VEC[n]
            return vecs[:, i:i + 1]

        for n in ("ssel", "ohalf", "tril8"):
            load(n)
        if 0 in layers:
            load("rt0")
            o = 0
            for n, sh in (("wq0", (1024,)), ("wk0", (512,)), ("wv0", (256,)), ("wo0", (8, P)), ("inp0", (384,)), ("outp0", (P,))):
                k = int(np.prod(sh))
                v = w0[:, o:o + k]
                W[n] = v if len(sh) == 1 else v.rearrange("p (a c) -> p a c", a=sh[0])
                L[n] = dma(n, W[n], d[n])
                o += k
            W["w1_0"] = wA[:, 0:2048].rearrange("p (e f) -> p e f", e=8)
            W["w2_0"] = wA[:, 2048:4096].rearrange("p (e f) -> p e f", e=16)
            for n in ("w1_0", "w2_0"):
                L[n] = dma(n, W[n], d[n])
        if 1 in layers:
            for n in ("mtri", "wqk1", "cos1", "sin1", "selq1", "selk1", "wvg1", "wo1", "lp1", "rt1"):
                load(n)
        if 2 in layers:
            for n in ("la2", "rt2", "rb2"):
                load(n)

        def late(names, where, col, waits):
            for n in names:
                k = d[n].shape[0]
                W[n] = where[0:k, col:col + P]
                L[n] = dma(n, W[n], d[n], waits)
                col += P

        xn = sb("xn", [P, NT])
        res = sb("res", [P, NT])
        pbuf = sb("pbuf", [P, 4, 2, T])
        tA = Ring([sb(f"tA{i}", [P, T])[:, :] for i in range(4)])
        tF = Ring([sb(f"tF{i}", [P, T])[:, :] for i in range(5)])
        tH = Ring([sb(f"tH{i}", [P, T])[:, :] for i in range(4)])
        tQ = Ring([sb(f"tQ{i}", [P, T])[:, :] for i in range(5)])
        tG = Ring([sb(f"tG{i}", [P, T])[:, :] for i in range(2)])
        small = Ring([sb(f"sm{i}", [P, 64])[:, :] for i in range(6)])
        state = {"x": [[Lx[b]] for b in range(NB)], "xnfree": [[] for _ in range(NB)]}
        xw = [Lx[b] for b in range(NB)]

        def cols(t, b):
            return t[:, b * T:(b + 1) * T]

        def spread(reps, ring, *waits, banks=misc):
            ex = ring.next()
            v = ex.ap.rearrange("p (t r) -> p t r", t=4)
            n, c = 0, None
            for src, rep in reps:
                k = src.shape[2]
                if rep > 0:
                    c = cp(v[:, :, n:n + k * rep].rearrange("p t (k r) -> p t k r", r=rep),
                           src.unsqueeze(3).to_broadcast([P, 4, k, rep]), waits, ex.free)
                else:
                    rep = -rep
                    c = cp(v[:, :, n:n + k * rep].rearrange("p t (r k) -> p t r k", r=rep),
                           src.unsqueeze(2).to_broadcast([P, 4, rep, k]), waits, ex.free)
                n += k * rep
            bk = banks.next()
            for t in range(4):
                m = tr(bk.ap[0:n, t * P:(t + 1) * P], v[:, t, 0:n], c, bk.free, L["ident"])
            ex.free = [m]
            return bk, m

        def rsqrt(x, y, z, *waits):
            xi, yi = x.bitcast(I32), y.bitcast(I32)
            a = op(DV, lambda e: e.tensor_scalar(yi, xi, 1, None, ALU.logical_shift_right), *waits)
            a = op(DV, lambda e: e.tensor_scalar(yi, yi, -1.0, float(0x5F3759DF), ALU.mult, ALU.add), a)
            for _ in range(3):
                a = tt(z, y, y, ALU.mult, a)
                a = stt(z, z, -0.5, x, ALU.mult, ALU.mult, a)
                a = stt(y, z, 1.5, y, ALU.add, ALU.mult, a)
            return a

        def here():
            return [Q.q[e][-1] for e in (PE, AC, DV, PO) if Q.q[e]]

        def lnorm(src, dst, waits, free=(), w=None, bb=None, eps=1e-5):
            b1 = misc.next()
            m = mm(b1.ap, W["ones"][:, :], src, True, True, b1.free, waits, L["ones"])
            xc = tt(dst, src, b1.ap, ALU.subtract, m, free)
            b1.free = [xc]
            s = tA.next()
            sq = act(s.ap, dst, ACT.Square, xc, s.free)
            yield
            b2 = misc.next()
            for t in range(4):
                v = mm(b2.ap[:, t:t + 1], s.ap[:, t * P:(t + 1) * P], W["ones"][:, 0:1], True, True, sq, b2.free)
            s.free = [v]
            st = small.next()
            e = ts(st.ap[:, 0:4], b2.ap[:, 0:4], eps, None, ALU.add, None, v, st.free)
            b2.free = [e]
            r = tt(st.ap[:, 4:8], st.ap[:, 0:4], W["ohalf"][:, 0:4], ALU.pow, e, L["ohalf"], eng=PO)
            yield
            bk, m = spread([(st.ap[:, 4:8].unsqueeze(2), P)], tA, r)
            st.free = [m]
            if w is None:
                o = tt(dst, dst, bk.ap, ALU.mult, m)
                bk.free = [o]
                return o
            o1 = stt(dst, dst, w, bk.ap, ALU.mult, ALU.mult, m, L["vecs"])
            bk.free = [o1]
            return ts(dst, dst, bb, None, ALU.add, None, o1)

        def softmax8(logits, w, g, ring):
            st = ring.next()
            m4 = st.ap[:, 0:4]
            mx = red(m4, logits, ALU.max, w, st.free)
            sub = tt(logits, logits, m4.unsqueeze(2).to_broadcast([P, 4, 8]), ALU.subtract, mx)
            ex = act(logits, logits, ACT.Exp, sub)
            sm = red(st.ap[:, 4:8], logits, ALU.add, ex)
            rc = rec(st.ap[:, 8:12], st.ap[:, 4:8], sm)
            o = tt(logits, logits, st.ap[:, 8:12].unsqueeze(2).to_broadcast([P, 4, 8]), ALU.mult, rc)
            st.free = [o]
            return o

        gst = sb("gst", [P, 4, 24])
        rk = sb("rk", [P, 32, 8])
        rk2 = sb("rk2", [P, 32, 8])
        gT = Ring([sb(f"gT{i}", [P, T], BF16)[:, :] for i in range(2)])
        gsplit = Ring([sb(f"gsp{i}", [P, 3, 32], BF16)[:, :, :] for i in range(2)])
        gz = [fill(gst[:, :, :], 0.0, eng=DV)]
        for bf in gT.bufs:
            bf.free = [fill(bf.ap, 0.0, eng=DV)]
        gfree = [gz]
        rkfree = [None]

        def route(src, waits, rt, top2, bias=None):
            bk = misc.next()
            for qt in range(4):
                m = mm(bk.ap[:, 8 * qt:8 * qt + 8], src[:, qt * P:(qt + 1) * P], W[rt][:, :], True, True,
                       waits, bk.free, L[rt])
            s = small.next()
            lg = s.ap[:, 0:32].rearrange("p (t e) -> p t e", e=8)
            bv = bk.ap[:, 0:32].rearrange("p (t e) -> p t e", e=8)
            if bias is None:
                c = cp(lg, bv, m, s.free)
            else:
                c = tt(lg, bv, W[bias][:, :].unsqueeze(1).to_broadcast([P, 4, 8]), ALU.add, m, s.free, L[bias])
            bk.free = [c]
            pr = softmax8(lg, c, None, small)
            flat = s.ap[:, 0:32]
            gs = gsplit.next()
            if top2:
                pj = lg.unsqueeze(2).to_broadcast([P, 4, 8, 8])
                pe_ = lg.unsqueeze(3).to_broadcast([P, 4, 8, 8])
                r1 = rk[:, :, :].rearrange("p (t e) j -> p t e j", e=8)
                r2 = rk2[:, :, :].rearrange("p (t e) j -> p t e j", e=8)
                a = [tt(r1[:, t], pj[:, t], pe_[:, t], ALU.is_equal, pr, rkfree) for t in range(4)][-1]
                a2 = tt(rk[:, :, :], rk[:, :, :], W["tril8"][:, :, :], ALU.mult, a, L["tril8"])
                a3 = [tt(r2[:, t], pj[:, t], pe_[:, t], ALU.is_gt, pr, rkfree) for t in range(4)][-1]
                a4 = tt(rk[:, :, :], rk[:, :, :], rk2[:, :, :], ALU.add, a2, a3)
                a5 = red(s.ap[:, 32:64], rk[:, :, :], ALU.add, a4)
                rkfree[0] = a5
                pr = stt(flat, s.ap[:, 32:64], 1.5, flat, ALU.is_lt, ALU.mult, a5)
            h = cp(gs.ap[:, 0, :], flat, pr, gs.free)
            gv = gst[:, :, 0:24].rearrange("p t (s e) -> p s t e", s=3)

            def col(k):
                return gv[:, k]

            hh = cp(col(0), gs.ap[:, 0, :].rearrange("p (t e) -> p t e", e=8), h, gfree)
            if top2:
                r = tt(flat, flat, gs.ap[:, 0, :], ALU.subtract, h)
                m1 = cp(gs.ap[:, 1, :], flat, r)
                cp(col(1), gs.ap[:, 1, :].rearrange("p (t e) -> p t e", e=8), m1)
                r = tt(flat, flat, gs.ap[:, 1, :], ALU.subtract, m1)
                hh = cp(col(2), lg, r)
            s.free = [hh]
            gs.free = [hh]
            bk = misc.next()
            for qt in range(4):
                m = tr(bk.ap[0:24, qt * P:(qt + 1) * P], gst[:, qt, :], hh, gz, bk.free, L["ident"])
            gfree[0] = m
            g = gT.next()
            c = cp(g.ap[0:24], bk.ap[0:24, :], m, g.free)
            bk.free = [c]
            return g, c

        def lockstep(gens):
            res_, on = [None] * len(gens), list(range(len(gens)))
            while on:
                for i in list(on):
                    try:
                        next(gens[i])
                    except StopIteration as e:
                        res_[i] = e.value
                        on.remove(i)
                yield
            return res_

        def weave(*streams):
            on = [[g, n, 0] for g, n in streams]
            while on:
                s = min(on, key=lambda v: (v[2] + 0.5) / v[1])
                s[2] += 1
                if next(s[0], "end") == "end":
                    on.remove(s)

        def chain(*gens):
            for g in gens:
                yield from g

        def layer0():
            av = arena[:, :]
            qsb = av[:, 0:4096].rearrange("p (a c) -> p a c", a=8)
            kA = av[:, 4096:6144].rearrange("p (a c) -> p a c", a=4)
            kB = av[:, 6144:8192].rearrange("p (a c) -> p a c", a=4)
            vsb = av[:, 8192:9216].rearrange("p (t c) -> p t c", t=4)
            qkv = av[:, 9216:15360].rearrange("p (b a c) -> p b a c", b=4, a=3)
            sc = av[:, 15360:17920].rearrange("p (a c) -> p a c", a=5)
            pt_ = [pbuf[:, i, j, :] for i in range(4) for j in range(2)]
            Sm = Ring([v.rearrange("p (a c) -> p a c", a=2) for v in pt_[0:5]])
            PTs = Ring(pt_[5:8])
            rq = Ring([sb(f"rq{i}", [P, 4, 16])[:, :, :] for i in range(2)])
            st2 = Ring([sb(f"st2{i}", [P, 8])[:, :] for i in range(8)])
            hn = res
            bS = Ring([A[0][:, 0, :], A[0][:, 1, :]])
            bT = Ring([A[1][:, 0, :], A[1][:, 1, :]])
            for bf in Sm.bufs:
                bf.free = [fill(bf.ap[:, :, 0:64], 0.0, eng=DV)]
            kz = [fill(kA[64:128, :, :], 0.0, eng=DV), fill(kB[0:64, :, :], 0.0, eng=DV)]
            wk = tt(vec("wqk"), vec("qn"), vec("kn"), ALU.mult, L["vecs"])
            wk = ts(vec("wqk"), vec("wqk"), 0.125, None, ALU.mult, None, wk)

            lnx = [None] * NB
            lnh2 = [None] * NB

            def norms():
                r = yield from lockstep([lnorm(cols(xT, b), cols(xn, b), state["x"][b]) for b in range(NB)])
                lnx[:] = r

            def pre():
                lnh = yield from lockstep([lnorm(cols(xn, b), cols(hn, b), lnx[b], w=vec("ln1w"), bb=vec("ln1b"))
                                           for b in range(NB)])
                ev = {}
                for b in range(NB):
                    for k in range(3):
                        bk = misc.next()
                        m = mm(bk.ap, W["inp0"][:, k * P:(k + 1) * P], cols(hn, b), True, True, lnh[b], bk.free, L["inp0"])
                        ev[b, k] = act(qkv[:, b, k, :], bk.ap, ACT.Identity, m, L["vecs"], bias=vec(f"inb{k}"))
                        bk.free = [ev[b, k]]
                        yield
                oW = {0: ev[0, 2]}
                oap = {0: qkv[:, 0, 2, :]}
                last_sc = None
                for s in range(1, NB):
                    prs = []
                    for t in range(s + 1):
                        tb = tF.next()
                        prs.append((tb, tt(tb.ap, qkv[:, s, 0, :], qkv[:, t, 1, :], ALU.mult, ev[s, 0], ev[t, 1], tb.free, eng=PO)))
                    scs = []
                    yield
                    for t in range(s + 1):
                        tb, pr = prs[t]
                        bk = misc.next()
                        m = mm(bk.ap, W["blk8"][:, :], tb.ap, True, True, pr, bk.free, L["blk8"])
                        tb.free = [m]
                        c = act(sc[:, t, :], bk.ap, ACT.Copy, m, last_sc, scale=1.0 / math.sqrt(8.0))
                        bk.free = [c]
                        scs.append(c)
                        yield
                    mx = tt(sc[:, 4, :], sc[:, 0, :], sc[:, 1, :], ALU.max, scs)
                    for t in range(2, s + 1):
                        mx = tt(sc[:, 4, :], sc[:, 4, :], sc[:, t, :], ALU.max, mx)
                    yield
                    exs = []
                    for t in range(s + 1):
                        u = tt(sc[:, t, :], sc[:, t, :], sc[:, 4, :], ALU.subtract, mx)
                        exs.append(act(sc[:, t, :], sc[:, t, :], ACT.Exp, u))
                    yield
                    sm = tt(sc[:, 4, :], sc[:, 0, :], sc[:, 1, :], ALU.add, exs)
                    for t in range(2, s + 1):
                        sm = tt(sc[:, 4, :], sc[:, 4, :], sc[:, t, :], ALU.add, sm)
                    yield
                    rc = rec(sc[:, 4, :], sc[:, 4, :], sm)
                    pv = []
                    for t in range(s + 1):
                        pv.append(tt(sc[:, t, :], sc[:, t, :], qkv[:, t, 2, :], ALU.mult, sm, ev[t, 2], eng=PO))
                    yield
                    ac = pv[0]
                    for t in range(1, s + 1):
                        ac = tt(sc[:, 0, :], sc[:, 0, :], sc[:, t, :], ALU.add, pv, ac)
                    oap[s] = qkv[:, s, 0, :]
                    oW[s] = tt(oap[s], sc[:, 0, :], sc[:, 4, :], ALU.mult, ac, rc)
                    last_sc = oW[s]
                    yield
                x1w = []
                for b in range(NB):
                    bk = misc.next()
                    m = mm(bk.ap, W["outp0"][:, :], oap[b], True, True, oW[b], bk.free, L["outp0"])
                    x1b = qkv[:, b, 1, :]
                    a = stt(x1b, bk.ap, vec("outb"), cols(xn, b), ALU.add, ALU.add, m, last_sc)
                    bk.free = [a]
                    xw[b] = tt(cols(xT, b), cols(xT, b), x1b, ALU.add, a, xw[b], lnx[b])
                    x1w.append(a)
                    yield
                r = yield from lockstep([lnorm(qkv[:, b, 1, :], cols(hn, b), x1w[b], w=vec("ln2w"), bb=vec("ln2b"))
                                         for b in range(NB)])
                lnh2[:] = r

            hist = {"q": [], "k": [], "v": []}

            def attn(b):
                X = cols(xn, b)
                ssb = bankO
                qe, sqs = [], []

                def sums(p):
                    s, sq = sqs[p]
                    j, i = p % 4, p // 4
                    ms = mm(ssb.ap[32 * j:32 * j + 32, :], W["ssel"][:, 32 * i:32 * i + 32], s.ap, i == 0, i == 1, sq,
                            ssb.free, L["ssel"])
                    s.free = [ms]
                    return ms

                for p in range(8):
                    bk = bS.next()
                    m = mm(bk.ap, W["wq0"][:, p * P:(p + 1) * P], X, True, True, lnx[b], bk.free, L["wq0"])
                    c = cp(qsb[:, p, :], bk.ap, m, hist["q"])
                    bk.free = [c]
                    qe.append(c)
                    s = tQ.next()
                    sqs.append((s, act(s.ap, qsb[:, p, :], ACT.Square, c, s.free)))
                    if p:
                        sums(p - 1)
                    yield
                bs = bT.next()
                kc = []
                for kv in range(4):
                    bk = bS.next()
                    m = mm(bk.ap, W["wk0"][:, kv * P:(kv + 1) * P], X, True, True, lnx[b], bk.free, L["wk0"])
                    if kv == 0:
                        ms = sums(7)
                    c1 = cp(kA[0:64, kv, :], bk.ap[0:64, :], m, hist["k"])
                    s = tQ.next()
                    sq = act(s.ap[64:128], bk.ap[64:128, :], ACT.Square, m, s.free)
                    c2 = act(kB[64:128, kv, :], bk.ap[64:128, :], ACT.Copy, m, hist["k"])
                    bk.free = [c1, c2]
                    kc.append((s, sq, c1, c2))
                    yield
                s = tQ.next()
                e = ts(s.ap, ssb.ap, 1.0 / 64, 1e-6, ALU.mult, ALU.add, ms, s.free)
                ssb.free = [e]
                for kv in range(4):
                    sk, sq, _, _ = kc[kv]
                    for t in range(4):
                        m = mm(bs.ap[:, 4 * kv + t:4 * kv + t + 1], sk.ap[64:128, t * P:(t + 1) * P], W["ssel"][64:128, 1:2],
                               True, True, sq, bs.free, L["ssel"])
                    sk.free = [m]
                st = small.next()
                e2 = ts(st.ap[:, 0:16], bs.ap[:, 0:16], 1.0 / 64, 1e-6, ALU.mult, ALU.add, m, st.free)
                bs.free = [e2]
                pw = tt(st.ap[:, 16:32], st.ap[:, 0:16], W["ohalf"][:, 0:16], ALU.pow, e2, L["ohalf"], eng=PO)
                bk = bT.next()
                for t in range(4):
                    m = tr(bk.ap[:, t * P:(t + 1) * P], s.ap[:, t * P:(t + 1) * P], e, bk.free, L["ident"])
                s.free = [m]
                r = rq.next()
                s2_ = small.next()
                s3_ = small.next()
                c = cp(s2_.ap.rearrange("p (t j i) -> p t j i", t=4, i=4),
                       bk.ap.rearrange("p (t j i) -> p t j i", t=4, j=4)[:, :, :, 0:4], m, s2_.free)
                bk.free = [c]
                rqw = rsqrt(s2_.ap, r.ap.rearrange("p t j -> p (t j)"), s3_.ap, c, r.free, s3_.free)
                s2_.free = s3_.free = [rqw]
                ve = []
                for t in range(4):
                    bk = bS.next()
                    m = mm(bk.ap[:, 0:256], X[:, t * P:(t + 1) * P], W["wv0"][:, :], True, True, lnx[b], bk.free, L["wv0"])
                    c = act(vsb[:, t, :], bk.ap[:, 0:256], ACT.Copy, m, hist["v"])
                    bk.free = [c]
                    ve.append(c)
                yield
                ke = []
                for kv in range(4):
                    _, _, c1, c2 = kc[kv]
                    bk, m = spread([(st.ap[:, 16 + 4 * kv:20 + 4 * kv].unsqueeze(2), P)], tQ, pw, banks=bT)
                    st.free = [m]
                    k1 = stt(kA[0:64, kv, :], kA[0:64, kv, :], vec("wqk")[0:64], bk.ap[0:64, :], ALU.mult, ALU.mult,
                             m, wk, c1, kz)
                    k2 = stt(kB[64:128, kv, :], kB[64:128, kv, :], vec("wqk")[64:128], bk.ap[64:128, :], ALU.mult,
                             ALU.mult, m, wk, c2, kz)
                    bk.free = [k2]
                    ke.append(k2)
                    yield
                ye = []
                work = [(p, t) for p in range(8) for t in range(4)]
                front = {}
                back = {}

                def scores(p, t):
                    kv = p // 2
                    w = 128 if t == 0 else 192
                    o = 256 - w
                    k0 = (t + 1) * P - w
                    S = bS.next()
                    for hf, kk in ((0, kA), (1, kB)):
                        m = mm(S.ap[:, 256 * hf:256 * hf + w], qsb[:, p, t * P:(t + 1) * P], kk[:, kv, k0:k0 + w], True, True,
                               S.free, qe[p], ke[kv])
                    sm = Sm.next()
                    st = st2.next()
                    for hf in range(2):
                        a = op(DV, lambda e, hf=hf: e.tensor_tensor_reduce(
                            sm.ap[:, hf, o:256], S.ap[:, 256 * hf:256 * hf + w], W["mband"][:, 192 - w:192], 1.0, -3e38,
                            ALU.add, ALU.max, st.ap[:, hf:hf + 1]), m, sm.free, st.free, L["mband"])
                    S.free = [a]
                    ix = (p % 4) * 4 + 2 * (p // 4)
                    nb = stt(st.ap[:, 2:4], st.ap[:, 0:2], -1.0, r.ap[:, t, ix:ix + 2], ALU.mult, ALU.mult, a, rqw)
                    for hf in range(2):
                        ex = act(sm.ap[:, hf, o:256], sm.ap[:, hf, o:256], ACT.Exp, nb, bias=st.ap[:, 2 + hf:3 + hf],
                                 scale=r.ap[:, t, ix + hf:ix + hf + 1], accum=st.ap[:, 4 + hf:5 + hf])
                    r.free = [ex]
                    front[p, t] = (sm, st, ex, w)

                def norm(p, t):
                    sm, st, ex, w = front[p, t]
                    o = 256 - w
                    rc = rec(st.ap[:, 6:8], st.ap[:, 4:6], ex)
                    nm = [ts(sm.ap[:, hf, o:256], sm.ap[:, hf, o:256], st.ap[:, 6 + hf:7 + hf], None, ALU.mult, None, rc,
                             eng=(DV, PO)[hf]) for hf in range(2)]
                    st.free = nm
                    front[p, t] = (sm, nm)

                def turn(p, t):
                    sm, nm = front[p, t]
                    nblk = 1 if t == 0 else 2
                    pt = bT.next()
                    for hf in range(2):
                        for k in range(nblk):
                            o = (hf * nblk + k) * P
                            c0 = (k + 2 - nblk) * P
                            m = tr(pt.ap[:, o:o + P], sm.ap[:, hf, c0:c0 + P], nm, pt.free, L["ident"])
                    sm.free = [m]
                    ps = PTs.next()
                    n = 2 * nblk * P
                    c = act(ps.ap[:, 0:n], pt.ap[:, 0:n], ACT.Copy, m, ps.free) if t % 2 else \
                        cp(ps.ap[:, 0:n], pt.ap[:, 0:n], m, ps.free)
                    pt.free = [c]
                    back[p, t] = (ps, c, nblk)

                def values(p, t):
                    ps, c, nblk = back[p, t]
                    kv = p // 2
                    for k in range(nblk):
                        for hf in range(2):
                            kb = t - nblk + 1 + k
                            o = (hf * nblk + k) * P
                            m = mm(bankO.ap[64 * hf:64 * hf + 64, t * P:(t + 1) * P], vsb[:, kb, kv * 64:kv * 64 + 64],
                                   ps.ap[:, o:o + P], k == 0, k == nblk - 1, c, ve, bankO.free if t == 0 else None)
                    ps.free = [m]
                    if t == 3:
                        yc = act(qsb[:, p, :], bankO.ap, ACT.Copy, m)
                        bankO.free = [yc]
                        ye.append(yc)
                    return m

                n = len(work)
                for i in range(n + 4):
                    if i < n:
                        scores(*work[i])
                    if 1 <= i <= n:
                        norm(*work[i - 1])
                    if 3 <= i < n + 3:
                        turn(*work[i - 3])
                    if i >= 4:
                        m = values(*work[i - 4])
                    yield
                hist["k"] = hist["v"] = [m]
                bk = bT.next()
                for p in range(8):
                    m = mm(bk.ap, W["wo0"][:, p, :], qsb[:, p, :], p == 0, p == 7, ye[p], bk.free, L["wo0"])
                hist["q"] = [m]
                xw[b] = tt(cols(xT, b), cols(xT, b), bk.ap, ALU.add, m, xw[b])
                bk.free = [xw[b]]
                yield

            def ffn(b):
                H = cols(hn, b)
                g, gw = route(H, lnh2[b], "rt0", True)
                yield
                y = bankY
                pend = []

                def down(k, h, gm):
                    m = mm(y.ap, W["w2_0"][:, k, :], h.ap, k == 0, k == 15, gm, y.free if k == 0 else None, L["w2_0"])
                    h.free = [m]
                    return m

                for e in range(8):
                    gb = misc.next()
                    gm = mm(gb.ap, W["selE"][:, e, :], g.ap, True, True, gw, gb.free, L["selE"])
                    gs = tG.next()
                    gc = cp(gs.ap, gb.ap, gm, gs.free)
                    gb.free = [gc]
                    new = []
                    for f in range(2):
                        bk = misc.next()
                        m = mm(bk.ap, W["w1_0"][:, e, f * P:(f + 1) * P], H, True, True, lnh2[b], bk.free, L["w1_0"])
                        h = tH.next()
                        a = act(h.ap, bk.ap, ACT.Gelu, m, h.free)
                        bk.free = [a]
                        k = tt(h.ap, h.ap, gs.ap, ALU.mult, a, gc, eng=PO)
                        new.append((2 * e + f, h, k))
                    gs.free = [k]
                    yield
                    for v in pend:
                        m = down(*v)
                    pend = new
                    yield
                g.free = [gm]
                for v in pend:
                    m = down(*v)
                xw[b] = tt(cols(xT, b), cols(xT, b), y.ap, ALU.add, m, xw[b])
                y.free = [xw[b]]
                yield

            weave((norms(), 1))
            weave((attn(0), 55), (pre(), 50))
            state["pre"] = here()
            for b in range(1, NB):
                weave((attn(b), 55), (ffn(b - 1), 18))
                settle(b - 1)
            for bf in pairs.bufs:
                bf.free = [bf_.free for bf_ in bS.bufs + bT.bufs]
            state["attn"] = here()
            return ffn(3)

        def settle(b):
            state["x"][b] = [xw[b]]
            state["xnfree"][b] = here()

        def halves(src, parts_, w, free, rows):
            t = tF.next()
            h = cp(parts_[0:rows, 0, :], src, w, free)
            r1 = tt(t.ap[0:rows], src, parts_[0:rows, 0, :], ALU.subtract, h, t.free)
            m = cp(parts_[0:rows, 1, :], t.ap[0:rows], r1)
            r2 = tt(t.ap[0:rows], t.ap[0:rows], parts_[0:rows, 1, :], ALU.subtract, m)
            lo = cp(parts_[0:rows, 2, :], t.ap[0:rows], r2)
            t.free = [lo]
            return lo

        qpart, kpart, mpart = (w0[:, 768 * k:768 * (k + 1)].bitcast(BF16).rearrange("p (s c) -> p s c", s=3) for k in range(3))
        junk = Ring([bf.ap.bitcast(BF16)[:, k * T:(k + 1) * T] for bf in tQ.bufs[2:4] for k in range(2)])
        mxr = Ring([sb(f"mx{i}", [P, 4, 32])[:, :, :] for i in range(2)])
        ytok = w0[:, 2304:2816].rearrange("p (t c) -> p t c", t=4)
        yst = Ring([sb(f"yst{i}", [P, 4, 4])[:, :, :] for i in range(2)])
        pb = Ring([pbuf[:, i, :, :] for i in range(4)])
        free = {"qpart": [], "kpart": [], "mpart": [], "ytok": [], "res": []}

        class Heads:

            def __init__(self, lay, D, GK, kof, bufs, vbufs, causal, padded):
                self.lay, self.D, self.GK, self.kof, self.causal, self.padded = lay, D, GK, kof, causal, padded
                self.J = 16 // D
                self.G = 8 * self.J
                self.rows = 96 + 3 * self.J
                self.q = [v[:, 0:8 * T].rearrange("p (g c) -> p g c", c=T) for v in bufs]
                self.k = [v[:, 8 * T:(8 + GK) * T].rearrange("p (g c) -> p g c", c=T) for v in bufs]
                self.v = vbufs
                self.dr = {k: [nc.dram_tensor(f"scr{lay}{k}{b}", (3, r, T), BF16, kind="Internal").ap() for b in range(NB)]
                           for k, r in (("q", P), ("k", P), ("m", self.G))}
                self.ready = [None, None]
                self.used = [[], []]

            def clear(self, i, w):
                a = []
                if not self.padded:
                    a.append(fill(self.k[i].rearrange("p g c -> p (g c)").bitcast(F32), 0.0, w))
                n = f"kone{self.lay}"
                c = dma(f"{n}_{i}", self.k[i][96:self.rows, :, :], d[n].bitcast(BF16), w, a)
                z = fill(self.v[i], 0.0, w)
                o = op(DV, lambda e: e.memset(self.v[i][:, :, :, self.D:self.D + 1], 1.0), z)
                self.ready[i] = [a, c, z, o]

        def stack(H, b, qw, kw):
            i, D, lay = b % 2, H.D, H.lay
            w1 = dma(f"wq{lay}{b}", H.dr["q"][b].rearrange("s r c -> r s c"), qpart, qw)
            w2 = dma(f"wk{lay}{b}", H.dr["k"][b].rearrange("s r c -> r s c"), kpart, kw)
            free["qpart"], free["kpart"] = [w1], [w2]
            for n, (a, k) in enumerate(zip(QT, KT)):
                r = slice(16 * n, 16 * n + 16)
                lq = dma(f"sq{lay}{b}", H.q[i][r], H.dr["q"][b][PART[a]].rearrange("(r g) c -> r g c", g=8), w1, H.used[i], H.ready[i])
                ks = H.dr["k"][b][PART[k]].rearrange("(r g) c -> r g c", g=8)
                if H.padded:
                    lk = dma(f"sk{lay}{b}", H.k[i][r], ks, w2, H.used[i], H.ready[i])
                else:
                    for j in range(H.J):
                        lk = dma(f"sk{lay}{b}", H.k[i][16 * n + D * j:16 * n + D * j + D, 8 * j:8 * j + 8, :], ks[D * j:D * j + D],
                                 w2, H.used[i], H.ready[i])
            return [lq, lk]

        def maxima(H, b, st):
            i = b % 2
            mx = mxr.next()
            last_ = None
            for g in range(0, H.G, 2):
                if H.causal:
                    for banks in (((0, 0, 0, 0), (0, 2, P, 0), (1, 0, 0, 1), (1, 2, P, 1)),
                                  ((0, 1, 0, 0), (1, 1, 2 * P, 0), (0, 3, 0, 1)), ((1, 3, 0, 0),)):
                        p1 = pairs.next()
                        ms = []
                        for k, t, o, bank in banks:
                            n = (t + 1) * P
                            ms.append(mm(p1.ap[:, bank, o:o + n], H.q[i][0:96, (g + k) % 8, t * P:(t + 1) * P],
                                         H.k[i][0:96, H.kof(g + k), 0:n], True, True, p1.free, st))
                        whole = {bank: m for (_, _, _, bank), m in zip(banks, ms)}
                        for k, t, o, bank in banks:
                            n = (t + 1) * P
                            jk = junk.next()
                            last_ = op(DV, lambda e, k=k, t=t, o=o, bank=bank, n=n, jk=jk, p1=p1, mx=mx, g=g:
                                       e.tensor_tensor_reduce(jk.ap[:, 0:n], p1.ap[:, bank, o:o + n], W["mtri"][:, T - n:T],
                                                              1.0, -3e38, ALU.add, ALU.max, mx.ap[:, t, g + k:g + k + 1]),
                                       whole[bank], jk.free, mx.free, L["mtri"])
                            jk.free = [last_]
                        p1.free = [last_]
                        yield None
                else:
                    for t in range(4):
                        p1 = pairs.next()
                        for k in (0, 1):
                            m = mm(p1.ap[:, k, :], H.q[i][0:96, (g + k) % 8, t * P:(t + 1) * P], H.k[i][0:96, H.kof(g + k), :],
                                   True, True, p1.free, st)
                        last_ = red(mx.ap[:, t, g:g + 2], p1.ap, ALU.max, m, mx.free)
                        p1.free = [last_]
                        yield None
            bk = misc.next()
            for t in range(4):
                m = tr(bk.ap[0:H.G, t * P:(t + 1) * P], mx.ap[:, t, 0:H.G], last_, bk.free, L["ident"])
            mx.free = [m]
            n_ = tF.next()
            ng = ts(n_.ap[0:H.G], bk.ap[0:H.G, :], -1.0, None, ALU.mult, None, m, n_.free)
            bk.free = [ng]
            lo = halves(n_.ap[0:H.G], mpart, ng, free["mpart"], H.G)
            n_.free = [lo]
            w1 = dma(f"wm{H.lay}{b}", H.dr["m"][b].rearrange("s r c -> r s c"), mpart[0:H.G, :, :], lo)
            free["mpart"] = [w1]
            l1 = dma(f"sm{H.lay}{b}", H.q[i][96:H.rows, :, :], H.dr["m"][b].rearrange("s (j g) c -> (s j) g c", g=8), w1)
            yield [l1]

        def weighted(H, b, tiles, st, ml, vw, put):
            i = b % 2
            steps = [(n, kb) for n in range(len(tiles)) for kb in range(4)]
            pend = None

            def flush(p):
                (n, kb), bufs, exs = p
                q0 = kb * P if H.causal else 0
                for j in range(4):
                    g, gv = tiles[n][j]
                    m = mm(bankO.ap[32 * j:32 * j + 32, q0:T], H.v[i][:, kb, gv, :], bufs[j // 2].ap[:, j % 2, 0:T - q0],
                           kb == 0, kb == 3, exs[j // 2], vw, bankO.free if kb == 0 else None)
                for bf in bufs:
                    bf.free = [m]
                if kb == 3:
                    o = tF.next()
                    oc = cp(o.ap, bankO.ap, m, o.free)
                    bankO.free = [oc]
                    bk = misc.next()
                    for t in range(4):
                        m2 = tr(bk.ap[:, t * P:(t + 1) * P], o.ap[:, t * P:(t + 1) * P], oc, bk.free, L["ident"])
                    o.free = [m2]
                    v = bk.ap.rearrange("p (t j r) -> p t j r", t=4, j=4)
                    s = yst.next()
                    rc = rec(s.ap, v[:, :, :, H.D], m2, s.free)
                    pw = put(n, v, s.ap, rc)
                    bk.free = [pw]
                    s.free = [pw]
                return m

            for n, kb in steps:
                q0 = kb * P if H.causal else 0
                bufs, exs = [], []
                for jj in range(2):
                    pr = pairs.next()
                    for k in range(2):
                        g, _ = tiles[n][2 * jj + k]
                        m = mm(pr.ap[:, k, 0:T - q0], H.k[i][0:H.rows, H.kof(g), kb * P:(kb + 1) * P],
                               H.q[i][0:H.rows, g % 8, q0:T],
                               True, not H.causal, pr.free, st, ml)
                        if H.causal:
                            m = mm(pr.ap[:, k, 0:P], identb, mdiagT, False, True, L["identb"], L["mdiagT"])
                    e = pb.next()
                    x = act(e.ap[:, :, 0:T - q0], pr.ap[:, :, 0:T - q0], ACT.Exp, m, e.free)
                    pr.free = [x]
                    bufs.append(e)
                    exs.append(x)
                if pend:
                    m = flush(pend)
                pend = ((n, kb), bufs, exs)
                yield
            m = flush(pend)
            H.used[i] = [m]
            yield

        identb, mdiagT = W["identb"][:, :], W["mdiagT"][:, :]

        def project_out(b, w, waits, bias=None, ytok=ytok):
            bk = misc.next()
            for t in range(4):
                m = tr(bk.ap[:, t * P:(t + 1) * P], ytok[:, t, :], waits, bk.free, L["ident"])
            free["ytok"] = [m]
            y = tA.next()
            c = act(y.ap, bk.ap, ACT.Copy, m, y.free)
            bk.free = [c]
            bk = misc.next()
            m = mm(bk.ap, W[w][:, :], y.ap, True, True, c, bk.free, L[w])
            y.free = [m]
            if bias is None:
                a = tt(cols(xT, b), cols(xT, b), bk.ap, ALU.add, m, xw[b])
            else:
                a = stt(cols(xT, b), bk.ap, vec(bias), cols(xT, b), ALU.add, ALU.add, m, xw[b])
            bk.free = [a]
            xw[b] = a

        def make1():
            a16 = arena[:, :].bitcast(BF16)
            at = (9216, 0)
            bufs = [a16[:, 2 * o:2 * o + 8192] for o in at]
            vb = [arena[:, o + 4096:o + 5120].rearrange("p (t g r) -> p t g r", t=4, g=8) for o in at]
            H = Heads(1, 4, 8, lambda h: h % 8 // 4 * 4 + h // 8, bufs, vb, True, True)
            tU = Ring([bf.ap for bf in tQ.bufs[0:2]])
            for bf in tU.bufs + junk.bufs:
                bf.free = [bf_.free for bf_ in tQ.bufs]
            rs = sb("rs1", [P, 3, 80])
            a1 = w0[:, 2816:3328].rearrange("p (s t c) -> p s t c", s=2, t=4)
            S = {}
            ftk = {"rs": [], "a1": []}
            for n, o, w in (("gw1", 14336, "pre"), ("uw1", 5120, "attn")):
                W[n] = arena[:, o:o + 2816]
                L[n] = dma(n, W[n], d[n], state[w])
            S["gain"] = ts(vec("gain"), vec("gain"), 0.5, None, ALU.mult, None, L["vecs"])

            def prep(b):
                if b < 2:
                    H.clear(b, here())
                yield
                X = cols(xn, b)
                lw = yield from lnorm(cols(xT, b), X, state["x"][b], state["xnfree"][b])
                S["ln", b] = lw
                yield
                rot, sqs = [], []
                for n in range(2):
                    o = 2 * n * P
                    bp = misc.next()
                    m = mm(bp.ap, W["wqk1"][:, o:o + P], X, True, True, lw, bp.free, L["wqk1"])
                    bs = misc.next()
                    m2 = mm(bs.ap, W["wqk1"][:, o + P:o + 2 * P], X, True, True, lw, bs.free)
                    u = tU.next()
                    u1 = tt(u.ap, bp.ap, W["cos1"][:, :], ALU.mult, m, u.free, L["cos1"])
                    s = tA.next()
                    sq = act(s.ap, bp.ap, ACT.Square, u1, s.free)
                    bp.free = [sq]
                    u2b = tF.next()
                    u2 = tt(u2b.ap, bs.ap, W["sin1"][:, :], ALU.mult, m2, u2b.free, L["sin1"])
                    bs.free = [u2]
                    u3 = tt(u.ap, u.ap, u2b.ap, ALU.add, u1, u2, eng=PO)
                    u2b.free = [u3]
                    rot.append((u, u3))
                    sqs.append((s, sq))
                    yield
                (u, u3), (k, k3) = rot
                (s, sq), (sk, sqk) = sqs
                bk = misc.next()
                for t in range(4):
                    mm(bk.ap[:, 20 * t:20 * t + 16], s.ap[:, t * P:(t + 1) * P], W["selq1"][:, :], True, True, sq, bk.free,
                       L["selq1"])
                    m = mm(bk.ap[:, 20 * t + 16:20 * t + 20], sk.ap[:, t * P:(t + 1) * P], W["selk1"][:, :], True, True,
                           sqk, L["selk1"])
                s.free = [m]
                sk.free = [m]
                e = ts(rs[:, 0, :], bk.ap[:, 0:80], float(np.finfo(np.float32).eps), None, ALU.add, None, m, ftk["rs"])
                bk.free = [e]
                yield
                r = rsqrt(rs[:, 0, :], rs[:, 1, :], rs[:, 2, :], e)
                yield
                bk = misc.next()
                for t in range(4):
                    m = mm(bk.ap[:, 64 * t:64 * t + 64], X[:, t * P:(t + 1) * P], W["wvg1"][:, :], True, True, lw, bk.free,
                           L["wvg1"])
                v4 = bk.ap[:, 0:256].rearrange("p (t s c) -> p t s c", t=4, s=2)
                tb = tF.next()
                th = act(tb.ap[:, 0:P].rearrange("p (t c) -> p t c", t=4), v4[:, :, 1, :], ACT.Tanh, m, tb.free, scale=0.5)
                g1 = stt(tb.ap[:, 0:P].rearrange("p (t c) -> p t c", t=4), tb.ap[:, 0:P].rearrange("p (t c) -> p t c", t=4),
                         1.0, v4[:, :, 0, :], ALU.add, ALU.mult, th)
                bk.free = [g1]
                vw = ts(H.v[b % 2][:, :, :, 0:4], tb.ap[:, 0:P].rearrange("p (t g i) -> p t g i", t=4, i=4), 0.5, None,
                        ALU.mult, None, g1, H.ready[b % 2], H.used[b % 2])
                tb.free = [vw]
                yield
                r3 = rs[:, 1, :].rearrange("p (t h) -> p t h", t=4)
                bk, m = spread([(r3[:, :, 4 * j:4 * j + 4], -8) for j in range(4)], tA, r)
                qw = stt(u.ap, u.ap, vec("gain"), bk.ap, ALU.mult, ALU.mult, m, u3, S["gain"])
                bk.free = [qw]
                qp = halves(u.ap, qpart, qw, free["qpart"], P)
                u.free = [qp]
                bk, m = spread([(r3[:, :, 16:20], 32)], tA, r)
                ftk["rs"] = [m]
                kw = tt(k.ap, k.ap, bk.ap, ALU.mult, m, k3)
                bk.free = [kw]
                kp = halves(k.ap, kpart, kw, free["kpart"], P)
                k.free = [kp]
                st = stack(H, b, qp, kp)
                for _ in range(10):
                    yield
                ml = None
                for x in maxima(H, b, st):
                    ml = x
                    yield
                S["in", b] = (st, ml, vw)

            def main(b):
                st, ml, vw = S["in", b]
                tiles = [[(8 * j + 4 * hf + r, 2 * j + hf) for j in range(4)] for hf in range(2) for r in range(4)]
                ws = []

                def put(n, v, rinv, rc):
                    hf, r = n // 4, n % 4
                    dst = a1[:, hf, :, :].rearrange("p t (j r i) -> p t j r i", j=4, r=4)[:, :, :, r, :]
                    o = tt(dst, v[:, :, :, 0:4], rinv.unsqueeze(3).to_broadcast([P, 4, 4, 4]), ALU.mult, rc, ftk["a1"])
                    ws.append(o)
                    return o

                for _ in weighted(H, b, tiles, st, ml, vw, put):
                    yield
                lp = W["lp1"][:, :].unsqueeze(1).to_broadcast([P, 4, 64])
                a = tt(a1[:, 1, :, :], a1[:, 1, :, :], lp, ALU.mult, ws, L["lp1"])
                y8 = ytok[:, :, :].rearrange("p t (h s i) -> p t h s i", s=2, i=4)
                A1 = a1[:, 0, :, :].rearrange("p t (h i) -> p t h i", i=4)
                A2 = a1[:, 1, :, :].rearrange("p t (h i) -> p t h i", i=4)
                yw = []
                for t in range(4):
                    yw.append(tt(y8[:, t, :, 0, :], A1[:, t], A2[:, t], ALU.subtract, a, free["ytok"]))
                    yw.append(tt(y8[:, t, :, 1, :], A1[:, t], A2[:, t], ALU.add, a, free["ytok"]))
                ftk["a1"] = yw
                project_out(b, "wo1", yw)
                yield

            def ffn(b):
                X = cols(xn, b)
                lw = S["ln", b]
                g, gw = route(X, lw, "rt1", True)
                yield
                y = bankY
                pend = []

                def down(k, M, h, w):
                    m = mm(y.ap, W["dw1"][0:M, k, :], h.ap[0:M], k == 0, k == 23, w, y.free if k == 0 else None, L["dw1"])
                    h.free = [m]
                    return m

                for e in range(8):
                    gb = misc.next()
                    gm = mm(gb.ap, W["selE"][:, e, :], g.ap, True, True, gw, gb.free, L["selE"])
                    xg = tG.next()
                    xgw = stt(xg.ap, X, 0.5, gb.ap, ALU.mult, ALU.mult, gm, lw, xg.free)
                    gb.free = [xgw]
                    for s, M in ((0, 128), (1, 128), (2, 96)):
                        o = e * 352 + s * P
                        bg = misc.next()
                        m1 = mm(bg.ap[0:M, :], W["gw1"][:, o:o + M], X, True, True, lw, bg.free, L["gw1"])
                        bu = misc.next()
                        m2 = mm(bu.ap[0:M, :], W["uw1"][:, o:o + M], xg.ap, True, True, xgw, bu.free, L["uw1"])
                        h = tH.next()
                        th = act(h.ap[0:M], bg.ap[0:M, :], ACT.Tanh, m1, h.free, scale=0.5)
                        h1 = stt(h.ap[0:M], h.ap[0:M], 1.0, bg.ap[0:M, :], ALU.add, ALU.mult, th)
                        bg.free = [h1]
                        h2 = tt(h.ap[0:M], h.ap[0:M], bu.ap[0:M, :], ALU.mult, h1, m2)
                        bu.free = [h2]
                        pend.append((3 * e + s, M, h, h2))
                        yield
                        if len(pend) > 1:
                            m = down(*pend.pop(0))
                        yield
                    xg.free = [m2]
                g.free = [gm]
                while pend:
                    m = down(*pend.pop(0))
                xw[b] = tt(cols(xT, b), cols(xT, b), y.ap, ALU.add, m, xw[b])
                y.free = [xw[b]]
                yield

            return prep, main, ffn

        def make2():
            a16 = arena[:, :].bitcast(BF16)
            bufs = [a16[:, 2 * o:2 * o + 12288] for o in (7936, 0)]
            vb = [v.rearrange("p (t g r) -> p t g r", t=4, g=16) for v in (res[:, :], arena[:, 14144:16192])]
            H = Heads(2, 8, 16, lambda h: h, bufs, vb, False, False)
            S = {}

            def prep(b):
                if b < 2:
                    H.clear(b, here())
                yield
                X = cols(xn, b)
                lw = yield from lnorm(cols(xT, b), X, state["x"][b], state["xnfree"][b])
                S["ln", b] = lw
                yield
                pw = []
                for w, bias, part, sc in (("wq2", "bq2", qpart, 1.0 / math.sqrt(8.0)), ("wk2", "bk2", kpart, 1.0)):
                    bk = misc.next()
                    m = mm(bk.ap, W[w][:, :], X, True, True, lw, bk.free, L[w])
                    t = tF.next()
                    c = ts(t.ap, bk.ap, vec(bias), sc, ALU.add, ALU.mult, m, t.free, L["vecs"])
                    bk.free = [c]
                    pw.append(halves(t.ap, part, c, free["qpart" if w == "wq2" else "kpart"], P))
                    t.free = [pw[-1]]
                    yield
                st = stack(H, b, pw[0], pw[1])
                bk = misc.next()
                for t in range(4):
                    m = mm(bk.ap[:, t * P:(t + 1) * P], X[:, t * P:(t + 1) * P], W["wv2"][:, :], True, True, lw, bk.free, L["wv2"])
                vw = []
                for t in range(4):
                    vw.append(tt(H.v[b % 2][:, t, :, 0:8], bk.ap[:, t * P:(t + 1) * P].rearrange("p (h i) -> p h i", i=8),
                                 W["bv2"][:, :].rearrange("p (h i) -> p h i", i=8), ALU.add, m, L["bv2"],
                                 H.ready[b % 2], H.used[b % 2]))
                bk.free = vw
                for _ in range(8):
                    yield
                ml = None
                for x in maxima(H, b, st):
                    ml = x
                    yield
                S["in", b] = (st, ml, vw)

            def main(b):
                st, ml, vw = S["in", b]
                tiles = [[(4 * r + j, 4 * r + j) for j in range(4)] for r in range(4)]
                ws = []

                def put(n, v, rinv, rc):
                    dst = ytok[:, :, :].rearrange("p t (n j i) -> p t n j i", n=4, i=8)[:, :, n, :, :]
                    o = tt(dst, v[:, :, :, 0:8], rinv.unsqueeze(3).to_broadcast([P, 4, 4, 8]), ALU.mult, rc, free["ytok"])
                    ws.append(o)
                    return o

                for _ in weighted(H, b, tiles, st, ml, vw, put):
                    yield
                project_out(b, "wo2", ws, "bo2")
                yield

            def ffn(b):
                X = cols(xn, b)
                lw = S["ln", b]
                g, gw = route(X, lw, "rt2", False, "rb2")
                yield
                bk = misc.next()
                m = mm(bk.ap[0:64, :], W["la2"][:, :], X, True, True, lw, bk.free, L["la2"])
                z = tH.next()
                c = act(z.ap[0:64], bk.ap[0:64, :], ACT.Copy, m, z.free, scale=2.0)
                bk.free = [c]
                bk = misc.next()
                m = mm(bk.ap[0:64, :], W["selR"][:, :], g.ap, True, True, gw, bk.free, L["selR"])
                g.free = [m]
                c = tt(z.ap[0:64], z.ap[0:64], bk.ap[0:64, :], ALU.mult, m, c)
                bk.free = [c]
                y = bankY
                mm(y.ap, W["base2"][:, :], X, True, False, lw, y.free, L["base2"])
                m = mm(y.ap, W["lb2"][:, :], z.ap[0:64], False, True, c, L["lb2"])
                z.free = [m]
                xw[b] = stt(cols(xT, b), y.ap, vec("bb2"), cols(xT, b), ALU.add, ALU.add, m, xw[b])
                y.free = [xw[b]]
                yield

            return prep, main, ffn

        def make3():
            S = {}
            toks = [arena[:, o:o + 1536].rearrange("p (t s c) -> p t s c", t=4, s=3) for o in (6144, 10240, 0, 2048)]
            s3s = [arena[:, o + 1536:o + 1856].rearrange("p (s c) -> p s c", s=5) for o in (6144, 10240, 0, 2048)]
            wide = [[arena[:, o + 1856 + T * k:o + 1856 + T * k + T] for k in range(4)] for o in (6144, 10240)]
            wide += [[pbuf[:, 2 * o + k // 2, k % 2, :] for k in range(4)] for o in range(2)]
            c3s = [sb(f"c3{b}", [P, 6, 16]) for b in range(NB)]
            kvms = [sb(f"kvm{b}", [P, P]) for b in range(NB)]
            yts = [w0[:, T * b:T * b + T].rearrange("p (t c) -> p t c", t=4) for b in range(NB)]
            hb = {n: ts(vec(n), vec(n), 0.5, None, ALU.mult, None, L["vecs"]) for n in ("bq3", "bk3")}
            wi = res[:, 0:1152].bitcast(I32)
            deq = ts(wA[:, 0:1152], wi, 1.0 / 127.0, None, ALU.mult, None, dma("wi3", wi, d["wi3"], here()))
            late(("wq3", "wk3", "wv3", "bv3", "wo3"), wA, 2048, here())
            EPS = 1e-6

            def prep(b):
                X = cols(xn, b)
                S["ln", b] = yield from lnorm(cols(xT, b), X, state["x"][b], state["xnfree"][b])
                yield

            def main(b):
                X = cols(xn, b)
                lw = S["ln", b]
                d_, dw = {}, {}
                tok, s3, c3, kvm, ytok = toks[b], s3s[b], c3s[b], kvms[b], yts[b]
                start = here()
                for n, (w, bias) in enumerate((("wq3", "bq3"), ("wk3", "bk3"))):
                    bk = misc.next()
                    m = mm(bk.ap, W[w][:, :], X, True, True, lw, bk.free, L[w])
                    t = Buf(wide[b][n])
                    a = act(t.ap, bk.ap, ACT.Tanh, m, hb[bias], start, bias=vec(bias), scale=0.5)
                    bk.free = [a]
                    yield
                    dw[n] = ts(t.ap, t.ap, 1.0, 0.5, ALU.add, ALU.mult, a)
                    d_[n] = t
                    sm = red(c3[:, 0, n:n + 1], t.ap, ALU.add, dw[n])
                    dw["s", n] = ts(c3[:, 0, n:n + 1], c3[:, 0, n:n + 1], EPS, None, ALU.add, None, sm)
                    bk = misc.next()
                    for q in range(4):
                        m = tr(bk.ap[:, q * P:(q + 1) * P], t.ap[:, q * P:(q + 1) * P], dw[n], bk.free, L["ident"])
                    dw["t", n] = cp(tok[:, :, n, :], bk.ap.rearrange("p (t c) -> p t c", t=4), m, start)
                    bk.free = [dw["t", n]]
                    te = Buf(wide[b][2 + n])
                    dw["e", n] = ts(te.ap, t.ap, EPS, None, ALU.add, None, dw[n], start)
                    d_["e", n] = te
                    yield
                bk = misc.next()
                for q in range(4):
                    m = mm(bk.ap[:, q * P:(q + 1) * P], X[:, q * P:(q + 1) * P], W["wv3"][:, :], True, True, lw, bk.free, L["wv3"])
                vw = tt(tok[:, :, 2, :], bk.ap.rearrange("p (t c) -> p t c", t=4),
                        W["bv3"][:, :].unsqueeze(1).to_broadcast([P, 4, P]), ALU.add, m, L["bv3"], start)
                bk.free = [vw]

                def dots(n, colsel, w, dst, f):
                    c = ts(c3[:, colsel, :], W["hsel"][:, :], c3[:, 0, n_of[colsel]:n_of[colsel] + 1], None, ALU.mult, None, w,
                           L["hsel"]) if colsel < 3 else w
                    bk = misc.next()
                    for q in range(4):
                        m = mm(bk.ap[:, 16 * q:16 * q + 16], d_["e", n].ap[:, q * P:(q + 1) * P], c3[:, colsel, :], True, True,
                               c, dw["e", n], bk.free)
                    o = f(dst, bk.ap[:, 0:64], m)
                    bk.free = [o]
                    return o

                n_of = {1: 1, 2: 0}
                si, so, cs, ce = s3[:, 0, :], s3[:, 1, :], s3[:, 2, :], s3[:, 3, :]
                w_si = dots(0, 1, dw["s", 1], si, lambda o, i_, m: rec(o, i_, m, start))
                w_so = dots(1, 2, dw["s", 0], so, lambda o, i_, m: rec(o, i_, m, start))
                yield
                w = {}
                for col_, n, st, ws in ((3, 1, so, w_so), (4, 0, si, w_si)):
                    bk = misc.next()
                    for q in range(4):
                        m = mm(bk.ap[:, 0:16], tok[:, q, n, :], st[:, 16 * q:16 * q + 16], q == 0, q == 3, ws, dw["t", n], bk.free)
                    a = ts(c3[:, col_, :], bk.ap[:, 0:16], EPS, None, ALU.add, None, m)
                    bk.free = [a]
                    w[col_] = tt(c3[:, col_, :], c3[:, col_, :], W["hsel"][:, :], ALU.mult, a, L["hsel"])
                w_cs = dots(0, 3, w[3], cs, lambda o, i_, m: act(o, i_, ACT.Exp, m, start, scale=-1.0))
                w_ce = dots(1, 4, w[4], ce, lambda o, i_, m: ts(o, i_, -1.0, 1.0, ALU.max, ALU.min, m, start))
                w_cs = ts(cs, cs, 1.0, None, ALU.add, None, w_cs)
                w_cs = rec(cs, cs, w_cs)
                w_cs = tt(cs, cs, si, ALU.mult, w_cs, w_si)
                w_ce = act(ce, ce, ACT.Exp, w_ce)
                bk = misc.next()
                m = mm(bk.ap[:, 0:64], W["ones"][:, :], ce, True, True, w_ce, bk.free, L["ones"])
                a = red(c3[:, 5, :], bk.ap[:, 0:64].rearrange("p (t h) -> p h t", t=4), ALU.add, m)
                bk.free = [a]
                a = rec(c3[:, 5, :], c3[:, 5, :], a)
                a = ts(c3[:, 5, :], c3[:, 5, :], float(T) / P, None, ALU.mult, None, a)
                sc = s3[:, 4, :]
                w_sc = tt(sc.rearrange("p (t h) -> p t h", t=4), ce.rearrange("p (t h) -> p t h", t=4),
                          c3[:, 5, :].unsqueeze(1).to_broadcast([P, 4, 16]), ALU.mult, a, w_ce)
                yield
                vs = []
                for q in range(4):
                    v3 = tok[:, q, 2, :].rearrange("p (h i) -> p h i", i=8)
                    vs.append(tt(v3, v3, sc[:, 16 * q:16 * q + 16].unsqueeze(2).to_broadcast([P, 16, 8]), ALU.mult, w_sc, vw))
                bk = misc.next()
                for q in range(4):
                    m = mm(bk.ap[:, 0:P], tok[:, q, 1, :], tok[:, q, 2, :], q == 0, q == 3, vs, dw["t", 1], bk.free)
                kw = tt(kvm[:, :], bk.ap[:, 0:P], W["blk8"][:, :], ALU.mult, m, L["blk8"])
                bk.free = [kw]
                bk = misc.next()
                for q in range(4):
                    m = mm(bk.ap[:, q * P:(q + 1) * P], d_[0].ap[:, q * P:(q + 1) * P], kvm[:, :], True, True, kw, bk.free)
                ys = []
                for q in range(4):
                    ys.append(tt(ytok[:, q, :].rearrange("p (h i) -> p h i", i=8),
                                 bk.ap[:, q * P:(q + 1) * P].rearrange("p (h i) -> p h i", i=8),
                                 cs[:, 16 * q:16 * q + 16].unsqueeze(2).to_broadcast([P, 16, 8]), ALU.mult, m, w_cs, start))
                bk.free = ys
                yield
                project_out(b, "wo3", ys, "bo3", ytok)
                yield

            def ffn(b):
                X = cols(xn, b)
                lw = S["ln", b]
                wg, wu, wd = wA[:, 0:384], wA[:, 384:768], wA[:, 768:1152]
                y = bankY
                for s in range(3):
                    bg = misc.next()
                    m1 = mm(bg.ap, wg[:, s * P:(s + 1) * P], X, True, True, lw, bg.free, deq)
                    bu = misc.next()
                    m2 = mm(bu.ap, wu[:, s * P:(s + 1) * P], X, True, True, lw, bu.free)
                    h = tH.next()
                    th = act(h.ap, bg.ap, ACT.Tanh, m1, h.free, scale=0.5)
                    h1 = stt(h.ap, h.ap, 1.0, bg.ap, ALU.add, ALU.mult, th)
                    bg.free = [h1]
                    h2 = stt(h.ap, h.ap, 0.5, bu.ap, ALU.mult, ALU.mult, h1, m2)
                    bu.free = [h2]
                    m = mm(y.ap, wd[:, s * P:(s + 1) * P], h.ap, s == 0, s == 2, h2, y.free if s == 0 else None)
                    h.free = [m]
                    yield
                xw[b] = tt(cols(xT, b), cols(xT, b), y.ap, ALU.add, m, xw[b])
                y.free = [xw[b]]
                yield

            return prep, main, ffn

        side = []
        state["pre"] = state["attn"] = []
        if 0 in layers:
            side = [(layer0(), 18)]
            for k in free:
                free[k] = state["attn"]
        if 1 in layers:
            prep, main, ffn = make1()
            weave((prep(0), 70), *side)
            if side:
                settle(3)
            W["dw1"] = wA[:, 0:3072].rearrange("p (e f) -> p e f", e=24)
            L["dw1"] = dma("dw1", W["dw1"], d["dw1"], here())
            side = []
        if 2 in layers:
            late(("wq2", "wk2", "wv2", "bv2", "wo2", "base2", "lb2"), wA, 3072, here())
            prep2, main2, ffn2 = make2()
        if 1 in layers:
            for b in range(NB):
                nxt = [(prep(b + 1), 84)] if b < 3 else [(prep2(0), 50)] if 2 in layers else []
                weave((main(b), 35), (ffn(b), 54), *nxt)
                settle(b)
        elif 2 in layers:
            weave((prep2(0), 50), *side)
            side = []
        if 2 in layers:
            for b in range(NB):
                if b < 3:
                    nxt = [(prep2(b + 1), 50)]
                elif 3 in layers:
                    prep3, main3, ffn3 = make3()
                    nxt = [(chain(ffn2(b), prep3(0), main3(0), ffn3(0)), 18), (chain(prep3(1), main3(1)), 12)]
                else:
                    nxt = []
                weave((main2(b), 19), *nxt, *([(ffn2(b), 3)] if b < 3 or not nxt else []))
                settle(b)
        if 3 in layers:
            if 2 in layers:
                weave((chain(prep3(2), main3(2)), 12), (chain(prep3(3), main3(3)), 12), (chain(ffn3(1), ffn3(2), ffn3(3)), 13))
            else:
                prep3, main3, ffn3 = make3()
                weave(*[(chain(prep3(b), main3(b)), 24) for b in range(NB)])
                weave((chain(*[ffn3(b) for b in range(NB)]), 1))
        elif side:
            weave(*side)

        for b in range(NB):
            fin = dma("out", out[:, b * T:(b + 1) * T], cols(xT, b), xw[b])
        op(SY, lambda e: e.nop(), fin)
        Q.emit()


VECS = ["ln1w", "ln1b", "ln2w", "ln2b", "inb0", "inb1", "inb2", "outb", "qn", "kn", "wqk",
        "gain", "bq2", "bk2", "bo2", "bb2", "bq3", "bk3", "bo3"]


def constants():
    c = {}

    def bf(a):
        return (np.ascontiguousarray(a, dtype=np.float32).view(np.uint32) >> 16).astype(np.uint16)

    i = np.arange(P)
    c["ident"] = np.eye(P, dtype=np.float32)
    c["identb"] = bf(np.eye(P))
    c["ones"] = np.full((P, P), 1.0 / P, np.float32)
    c["ohalf"] = np.full((P, 16), -0.5, np.float32)
    c["blk8"] = (i[:, None] // 8 == i[None] // 8).astype(np.float32)
    j = np.arange(192)
    dist = i[:, None] + 64 - j[None]
    c["mband"] = np.where((dist >= 0) & (dist < 64), 0.0, NEG).astype(np.float32)
    c["mtri"] = np.zeros((P, T), np.float32)
    c["mtri"][:, 3 * P:T] = np.where(i[None] <= i[:, None], 0.0, NEG)
    c["mdiagT"] = bf(np.where(i[:, None] <= i[None], 0.0, NEG))
    sel = np.zeros((P, 8, P), np.float32)
    for e in range(8):
        sel[[e, 8 + e, 16 + e], e, :] = 1
    c["selE"] = bf(sel)
    s = np.zeros((P, 64), np.float32)
    for e in range(8):
        s[e, 8 * e:8 * e + 8] = 1
    c["selR"] = bf(s)
    ss = np.zeros((P, 2, 32), np.float32)
    for k in range(2):
        ss[0:64, k, 2 * k] = 1
        ss[64:128, k, 2 * k + 1] = 1
    c["ssel"] = ss.reshape(P, 64)
    tl = (np.arange(8)[None] < np.arange(8)[:, None]).astype(np.float32)
    c["tril8"] = np.ascontiguousarray(np.broadcast_to(np.tile(tl, (4, 1))[None], (P, 32, 8)))
    pi = i // 8 % 4
    ang = (np.arange(0, 8, 2, dtype=np.float32) / np.float32(8) * np.float32(math.pi)).astype(np.float32)
    pos = np.arange(T, dtype=np.float32)
    rad = (np.float32(1) / (np.float32(1) + pos * np.float32(0.01))).astype(np.float32)
    a = (pos[:, None] * ang[None]).astype(np.float32)
    co = (rad[:, None] * np.cos(a)).astype(np.float32).T
    si = (rad[:, None] * np.sin(a)).astype(np.float32).T
    c["cos1"] = np.ascontiguousarray(co[pi])
    c["sin1"] = np.ascontiguousarray(np.where((i % 8 < 4)[:, None], si[pi], -si[pi]))
    c["selq1"] = ((i // 32 * 4 + i % 4)[:, None] == np.arange(16)[None]) * np.float32(1 / 8)
    c["selk1"] = ((i // 32)[:, None] == np.arange(4)[None]) * np.float32(1 / 8)
    c["selq1"], c["selk1"] = c["selq1"].astype(np.float32), c["selk1"].astype(np.float32)
    one = np.zeros((3, 4, 8, T), np.float32)
    for h in range(8):
        one[:, h % 4, h] = 1
    c["kone1"] = bf(one.reshape(12, 8, T))
    one = np.zeros((3, 2, 16, T), np.float32)
    for h in range(16):
        one[:, h // 8, h] = 1
    c["kone2"] = bf(one.reshape(6, 16, T))
    c["hsel"] = (i[:, None] // 8 == np.arange(16)[None]).astype(np.float32)
    return c


def layout(x):
    f = {}

    def T_(a):
        return np.ascontiguousarray(np.asarray(a).T)

    f["xT"] = T_(np.asarray(x["L0_attn_x"]).reshape(NT, P))
    f["wq0"] = T_(x["L0_attn_wq"])
    k = np.asarray(x["L0_attn_wk"]).reshape(4, 1, 64, P)
    f["wk0"] = T_(np.concatenate([k, k], 1).reshape(512, P))
    f["wv0"] = T_(x["L0_attn_wv"])
    f["wo0"] = np.ascontiguousarray(np.asarray(x["L0_attn_wo"]).T.reshape(8, P, P).transpose(1, 0, 2))
    f["inp0"] = T_(x["L0_ffn_in_proj_w"])
    f["outp0"] = T_(x["L0_ffn_out_proj_w"])
    f["rt0"] = T_(x["L0_ffn_router_w"])
    f["w1_0"] = np.ascontiguousarray(np.asarray(x["L0_ffn_w1"]).transpose(1, 0, 2))
    f["w2_0"] = np.ascontiguousarray(np.asarray(x["L0_ffn_w2"]).reshape(16, P, P).transpose(1, 0, 2))
    v = np.zeros((P, len(VECS)), np.float32)

    def put(n, a):
        v[:, VECS.index(n)] = np.asarray(a)

    put("ln1w", x["L0_ffn_ln1_w"])
    put("ln1b", x["L0_ffn_ln1_b"])
    put("ln2w", x["L0_ffn_ln2_w"])
    put("ln2b", x["L0_ffn_ln2_b"])
    for k in range(3):
        put(f"inb{k}", np.asarray(x["L0_ffn_in_proj_b"])[k * P:(k + 1) * P])
    put("outb", x["L0_ffn_out_proj_b"])
    put("qn", np.tile(np.asarray(x["L0_attn_q_norm_w"]), 2))
    put("kn", np.tile(np.asarray(x["L0_attn_k_norm_w"]), 2))
    put("gain", np.broadcast_to(np.asarray(x["L1_attn_q_gain"]).reshape(4, 1, 1, 4), (4, 4, 2, 4)).reshape(P))
    o2 = np.arange(P).reshape(2, 8, 8).transpose(0, 2, 1).reshape(P)
    put("bq2", np.asarray(x["L2_attn_bq"])[o2])
    put("bk2", np.asarray(x["L2_attn_bk"])[o2])
    f["wq2"] = T_(np.asarray(x["L2_attn_Wq"])[o2])
    f["wk2"] = T_(np.asarray(x["L2_attn_Wk"])[o2])
    for n, s in (("bo2", "L2_attn_bo"), ("bb2", "L2_ffn_base_b"),
                 ("bq3", "L3_attn_bq"), ("bk3", "L3_attn_bk"), ("bo3", "L3_attn_bo")):
        put(n, x[s])
    f["vecs"] = v

    def rep(a):
        return np.ascontiguousarray(np.broadcast_to(np.asarray(a).reshape(1, -1), (P, np.asarray(a).size)))

    wq = np.asarray(x["L1_attn_Wq"]).reshape(4, 4, 2, 4, P).transpose(0, 3, 2, 1, 4)
    wk = np.zeros((4, 4, 2, 4, P), np.float32)
    for j in range(4):
        wk[j, :, :, j] = np.asarray(x["L1_attn_Wk"]).reshape(4, 2, 4, P)[j].transpose(1, 0, 2)
    f["wqk1"] = T_(np.concatenate([w.reshape(P, P) for w in (wq, wq[:, :, ::-1], wk, wk[:, :, ::-1])]))
    f["wvg1"] = T_(np.concatenate([np.asarray(x["L1_attn_Wv"]), np.asarray(x["L1_attn_Wg"])]))
    f["wo1"] = T_(x["L1_attn_Wo"])
    f["lp1"] = rep(np.repeat(np.asarray(x["L1_attn_lambda_param"]), 4))
    f["rt1"] = T_(x["L1_ffn_router_w"])
    f["gw1"] = T_(np.asarray(x["L1_ffn_gate_w"]).reshape(-1, P))
    f["uw1"] = T_(np.asarray(x["L1_ffn_up_w"]).reshape(-1, P))
    dw = np.zeros((8, 384, P), np.float32)
    dw[:, 0:352] = np.asarray(x["L1_ffn_down_w"]).transpose(0, 2, 1)
    f["dw1"] = np.ascontiguousarray(dw.reshape(24, P, P).transpose(1, 0, 2))
    for n, s in (("wv2", "L2_attn_Wv"), ("wo2", "L2_attn_Wo"),
                 ("base2", "L2_ffn_base_w"), ("rt2", "L2_ffn_router_w"),
                 ("wq3", "L3_attn_Wq"), ("wk3", "L3_attn_Wk"), ("wv3", "L3_attn_Wv"), ("wo3", "L3_attn_Wo")):
        f[n] = T_(x[s])
    f["bv2"] = rep(x["L2_attn_bv"])
    f["bv3"] = rep(x["L3_attn_bv"])
    f["rb2"] = rep(x["L2_ffn_router_b"])
    f["la2"] = np.ascontiguousarray(np.tile(np.asarray(x["L2_ffn_lora_A"]), (1, 8)))
    f["lb2"] = np.ascontiguousarray(np.asarray(x["L2_ffn_lora_B"]).reshape(64, P))
    wd = np.asarray(x["L3_ffn_w_down"]).T.reshape(3, P, P).transpose(1, 0, 2).reshape(P, 384)
    f["wi3"] = np.ascontiguousarray(np.concatenate([np.asarray(x["L3_ffn_w_gate"]).T, np.asarray(x["L3_ffn_w_up"]).T, wd], 1))
    return f


def kernel(_layers=(0, 1, 2, 3), **inputs):
    import concourse.bacc as bacc
    from concourse.bass_utils import run_bass_kernel_spmd as run

    nc = bacc.Bacc("TRN2", target_bir_lowering=False, num_devices=1)
    arrays = {**constants(), **layout(inputs)}
    d = {n: nc.dram_tensor("in_" + n, a.shape, mybir.dt.from_np(a.dtype), kind="ExternalInput").ap()
         for n, a in arrays.items()}
    out = nc.dram_tensor("out_x", (P, NT), F32, kind="ExternalOutput").ap()
    build(nc, d, out, _layers)
    r = run(nc, [{"in_" + n: a for n, a in arrays.items()}], core_ids=[0])
    return np.ascontiguousarray(np.asarray(r.results[0]["out_x"]).T).reshape(NB, T, P)
```
